# Optimizing a Trainium2 kernel written in Bass

```python
import numpy as np
import jax
import jax.numpy as jnp

def _softmax(x, axis=-1):
    return jax.nn.softmax(x, axis=axis)

def _gelu(x):
    return jax.nn.gelu(x, approximate=True)

def _silu(x):
    return jax.nn.silu(x)

def _sigmoid(x):
    return jax.nn.sigmoid(x)

def _layernorm(x, axis=-1, eps=1e-05):
    m = jnp.mean(x, axis=axis, keepdims=True)
    v = jnp.var(x, axis=axis, keepdims=True)
    return (x - m) / jnp.sqrt(v + eps)

def _scatter_add(tgt, idx, src, axis=0):
    return tgt.at[idx].add(src)

def _segment_sum(src, seg, n):
    return jax.ops.segment_sum(src, seg, n)
kernel_name = 'mk_seq_preln_d1_jaxref_r8_59a183'

def setup_inputs(seed: int=0):
    np.random.seed(seed)
    _w = jnp.asarray

    def _L0_attn_setup():
        import jax, jax.numpy as jnp
        import numpy as np
        B, S, E, H, D = (4, 256, 128, 16, 64)

        def _large_negative_number(dtype):
            return jnp.asarray(-0.7 * jnp.finfo(dtype).max, dtype=dtype)
        key = jax.random.key(seed)
        k1, k2, k3 = jax.random.split(key, 3)
        x = jax.random.normal(k1, (B, S, E), dtype=jnp.float32)
        qkv_w = jax.random.normal(k2, (E, H, 3 * D), dtype=jnp.float32) * (1.0 / np.sqrt(E))
        qkv_b = jnp.zeros((H, 3 * D), dtype=jnp.float32)
        out_w = jax.random.normal(k3, (H, D, E), dtype=jnp.float32) * (1.0 / np.sqrt(H * D))
        out_b = jnp.zeros((E,), dtype=jnp.float32)
        return {'x': x, 'qkv_w': qkv_w, 'qkv_b': qkv_b, 'out_w': out_w, 'out_b': out_b}
    _L0_attn_in = _L0_attn_setup()

    def _L0_ffn_setup():
        import jax, jax.numpy as jnp
        import numpy as np
        DIM = 128
        DEPTH = 6
        HEADS = 16
        DIM_HEAD = 64
        WINDOW = 32
        INNER = HEADS * DIM_HEAD
        DIM_INNER = int(DIM * 4 * 2 / 3)
        QK_SCALE = 8.0

        def shift_tokens(t):
            a, s = jnp.split(t, 2, -1)
            s = jnp.pad(s, ((0, 0), (1, 0), (0, 0)))[:, :-1]
            return jnp.concatenate([a, s], -1)

        def l2norm(t):
            return t / jnp.maximum(jnp.linalg.norm(t, axis=-1, keepdims=True), 1e-12)

        def rotate_half(x):
            x1, x2 = jnp.split(x, 2, -1)
            return jnp.concatenate([-x2, x1], -1)

        def rotary_tables(n):
            half = jnp.arange(0, DIM_HEAD, 2, dtype=jnp.float32)
            inv_freq = 1.0 / 10000.0 ** (half / DIM_HEAD)
            t = jnp.arange(n, dtype=jnp.float32)
            freqs = t[:, None] * inv_freq[None, :]
            freqs = jnp.concatenate([freqs, freqs], -1)
            base_scale = (half + 0.4 * DIM_HEAD) / (1.4 * DIM_HEAD)
            power = (t - n // 2) / (WINDOW // 2)
            scale = base_scale[None, :] ** power[:, None]
            scale = jnp.concatenate([scale, scale], -1)
            return (freqs, scale)

        def local_attention(q, k, v):
            b, h, n, d = q.shape
            w = WINDOW
            nw = n // w
            bq = q.reshape(b, h, nw, w, d)
            bk = k.reshape(b, h, nw, w, d)
            bv = v.reshape(b, h, nw, w, d)

            def look(t):
                p = jnp.pad(t, ((0, 0), (0, 0), (1, 0), (0, 0), (0, 0)))
                return jnp.concatenate([p[:, :, :nw], p[:, :, 1:]], axis=3)
            bk2, bv2 = (look(bk), look(bv))
            seq = jnp.arange(n).reshape(nw, w)
            seq_p = jnp.pad(seq, ((1, 0), (0, 0)), constant_values=-1)
            jt = jnp.concatenate([seq_p[:nw], seq_p[1:]], axis=1)
            it = seq[:, :, None]
            jb = jt[:, None, :]
            mask = (it < jb) | (it > jb + w) | (jb == -1)
            sim = jnp.einsum('bhwie,bhwje->bhwij', bq, bk2) * QK_SCALE
            sim = jnp.where(mask, -jnp.finfo(sim.dtype).max, sim)
            attn = jax.nn.softmax(sim, -1)
            out = jnp.einsum('bhwij,bhwje->bhwie', attn, bv2)
            return out.reshape(b, h, n, d)

        def attn_layer(x, Wqkv, qs, ksc, Wo):
            b, n, _ = x.shape
            qkv = x @ Wqkv
            q, k, v = jnp.split(qkv, 3, -1)
            sh = lambda t: t.reshape(b, n, HEADS, DIM_HEAD).transpose(0, 2, 1, 3)
            q, k, v = (sh(q), sh(k), sh(v))
            q = l2norm(q) * qs
            k = l2norm(k) * ksc
            freqs, scale = rotary_tables(n)
            cos, sin = (jnp.cos(freqs), jnp.sin(freqs))
            q = q * cos * scale + rotate_half(q) * sin * scale
            inv = 1.0 / scale
            k = k * cos * inv + rotate_half(k) * sin * inv
            out = local_attention(q, k, v)
            out = out.transpose(0, 2, 1, 3).reshape(b, n, INNER)
            return out @ Wo

        def ffn_layer(x, g, bln, W1, b1, W2, b2):
            mu = x.mean(-1, keepdims=True)
            var = ((x - mu) ** 2).mean(-1, keepdims=True)
            xn = (x - mu) / jnp.sqrt(var + 1e-05) * g + bln
            hg = xn @ W1 + b1
            a, gate = jnp.split(hg, 2, -1)
            return a * jax.nn.gelu(gate, approximate=False) @ W2 + b2
        key = jax.random.key(seed)
        ks = jax.random.split(key, 8)
        B, N = (2, 256)
        init = lambda k, shape: jax.random.normal(k, shape, jnp.float32) * 0.02
        return {'x': jax.random.normal(ks[0], (B, N, DIM), jnp.float32), 'Wqkv': init(ks[1], (DEPTH, DIM, 3 * INNER)), 'q_scale': jnp.ones((DEPTH, DIM_HEAD), jnp.float32), 'k_scale': jnp.ones((DEPTH, DIM_HEAD), jnp.float32), 'Wo': init(ks[2], (DEPTH, INNER, DIM)), 'ln_g': jnp.ones((DEPTH, DIM), jnp.float32), 'ln_b': jnp.zeros((DEPTH, DIM), jnp.float32), 'W1': init(ks[3], (DEPTH, DIM, 2 * DIM_INNER)), 'b1': jnp.zeros((DEPTH, 2 * DIM_INNER), jnp.float32), 'W2': init(ks[4], (DEPTH, DIM_INNER, DIM)), 'b2': jnp.zeros((DEPTH, DIM), jnp.float32)}
    _L0_ffn_in = _L0_ffn_setup()
    _d = {'L0_attn_x': _L0_attn_in['x'], 'L0_attn_qkv_w': _L0_attn_in['qkv_w'], 'L0_attn_qkv_b': _L0_attn_in['qkv_b'], 'L0_attn_out_w': _L0_attn_in['out_w'], 'L0_attn_out_b': _L0_attn_in['out_b'], 'L0_ffn_Wqkv': _L0_ffn_in['Wqkv'], 'L0_ffn_q_scale': _L0_ffn_in['q_scale'], 'L0_ffn_k_scale': _L0_ffn_in['k_scale'], 'L0_ffn_Wo': _L0_ffn_in['Wo'], 'L0_ffn_ln_g': _L0_ffn_in['ln_g'], 'L0_ffn_ln_b': _L0_ffn_in['ln_b'], 'L0_ffn_W1': _L0_ffn_in['W1'], 'L0_ffn_b1': _L0_ffn_in['b1'], 'L0_ffn_W2': _L0_ffn_in['W2'], 'L0_ffn_b2': _L0_ffn_in['b2']}
    _x0 = _d['L0_attn_x']
    _d['L0_attn_x'] = jax.random.normal(jax.random.fold_in(jax.random.key(seed), 1), (8, 512, 128), dtype=_x0.dtype)
    del _x0
    return _d

def reference(L0_attn_x, L0_attn_qkv_w, L0_attn_qkv_b, L0_attn_out_w, L0_attn_out_b, L0_ffn_Wqkv, L0_ffn_q_scale, L0_ffn_k_scale, L0_ffn_Wo, L0_ffn_ln_g, L0_ffn_ln_b, L0_ffn_W1, L0_ffn_b1, L0_ffn_W2, L0_ffn_b2):

    def _L0_attn_ref(x, qkv_w, qkv_b, out_w, out_b):
        import jax, jax.numpy as jnp
        import numpy as np
        B, S, E, H, D = (4, 256, 128, 16, 64)

        def _large_negative_number(dtype):
            return jnp.asarray(-0.7 * jnp.finfo(dtype).max, dtype=dtype)
        qkv = jnp.einsum('bse,ehd->bshd', x, qkv_w) + qkv_b
        q, k, v = jnp.split(qkv, 3, axis=-1)
        logits = jnp.einsum('bqhd,bkhd->bhqk', q, k)
        logits = logits / jnp.sqrt(jnp.asarray(q.shape[-1], logits.dtype))
        mask = jnp.tril(jnp.ones((q.shape[1], q.shape[1]), dtype=jnp.bool_))
        logits = jnp.where(mask, logits, _large_negative_number(logits.dtype))
        probs = jax.nn.softmax(logits, axis=-1)
        attn = jnp.einsum('bhqk,bkhd->bqhd', probs, v)
        return jnp.einsum('bqhd,hde->bqe', attn, out_w) + out_b

    def _L0_ffn_ref(x, Wqkv, q_scale, k_scale, Wo, ln_g, ln_b, W1, b1, W2, b2):
        import jax, jax.numpy as jnp
        import numpy as np
        DIM = 128
        DEPTH = 6
        HEADS = 16
        DIM_HEAD = 64
        WINDOW = 32
        INNER = HEADS * DIM_HEAD
        DIM_INNER = int(DIM * 4 * 2 / 3)
        QK_SCALE = 8.0

        def shift_tokens(t):
            a, s = jnp.split(t, 2, -1)
            s = jnp.pad(s, ((0, 0), (1, 0), (0, 0)))[:, :-1]
            return jnp.concatenate([a, s], -1)

        def l2norm(t):
            return t / jnp.maximum(jnp.linalg.norm(t, axis=-1, keepdims=True), 1e-12)

        def rotate_half(x):
            x1, x2 = jnp.split(x, 2, -1)
            return jnp.concatenate([-x2, x1], -1)

        def rotary_tables(n):
            half = jnp.arange(0, DIM_HEAD, 2, dtype=jnp.float32)
            inv_freq = 1.0 / 10000.0 ** (half / DIM_HEAD)
            t = jnp.arange(n, dtype=jnp.float32)
            freqs = t[:, None] * inv_freq[None, :]
            freqs = jnp.concatenate([freqs, freqs], -1)
            base_scale = (half + 0.4 * DIM_HEAD) / (1.4 * DIM_HEAD)
            power = (t - n // 2) / (WINDOW // 2)
            scale = base_scale[None, :] ** power[:, None]
            scale = jnp.concatenate([scale, scale], -1)
            return (freqs, scale)

        def local_attention(q, k, v):
            b, h, n, d = q.shape
            w = WINDOW
            nw = n // w
            bq = q.reshape(b, h, nw, w, d)
            bk = k.reshape(b, h, nw, w, d)
            bv = v.reshape(b, h, nw, w, d)

            def look(t):
                p = jnp.pad(t, ((0, 0), (0, 0), (1, 0), (0, 0), (0, 0)))
                return jnp.concatenate([p[:, :, :nw], p[:, :, 1:]], axis=3)
            bk2, bv2 = (look(bk), look(bv))
            seq = jnp.arange(n).reshape(nw, w)
            seq_p = jnp.pad(seq, ((1, 0), (0, 0)), constant_values=-1)
            jt = jnp.concatenate([seq_p[:nw], seq_p[1:]], axis=1)
            it = seq[:, :, None]
            jb = jt[:, None, :]
            mask = (it < jb) | (it > jb + w) | (jb == -1)
            sim = jnp.einsum('bhwie,bhwje->bhwij', bq, bk2) * QK_SCALE
            sim = jnp.where(mask, -jnp.finfo(sim.dtype).max, sim)
            attn = jax.nn.softmax(sim, -1)
            out = jnp.einsum('bhwij,bhwje->bhwie', attn, bv2)
            return out.reshape(b, h, n, d)

        def attn_layer(x, Wqkv, qs, ksc, Wo):
            b, n, _ = x.shape
            qkv = x @ Wqkv
            q, k, v = jnp.split(qkv, 3, -1)
            sh = lambda t: t.reshape(b, n, HEADS, DIM_HEAD).transpose(0, 2, 1, 3)
            q, k, v = (sh(q), sh(k), sh(v))
            q = l2norm(q) * qs
            k = l2norm(k) * ksc
            freqs, scale = rotary_tables(n)
            cos, sin = (jnp.cos(freqs), jnp.sin(freqs))
            q = q * cos * scale + rotate_half(q) * sin * scale
            inv = 1.0 / scale
            k = k * cos * inv + rotate_half(k) * sin * inv
            out = local_attention(q, k, v)
            out = out.transpose(0, 2, 1, 3).reshape(b, n, INNER)
            return out @ Wo

        def ffn_layer(x, g, bln, W1, b1, W2, b2):
            mu = x.mean(-1, keepdims=True)
            var = ((x - mu) ** 2).mean(-1, keepdims=True)
            xn = (x - mu) / jnp.sqrt(var + 1e-05) * g + bln
            hg = xn @ W1 + b1
            a, gate = jnp.split(hg, 2, -1)
            return a * jax.nn.gelu(gate, approximate=False) @ W2 + b2
        for i in range(DEPTH):
            x = attn_layer(shift_tokens(x), Wqkv[i], q_scale[i], k_scale[i], Wo[i]) + x
            x = ffn_layer(shift_tokens(x), ln_g[i], ln_b[i], W1[i], b1[i], W2[i], b2[i]) + x
        return x
    x = L0_attn_x
    x = x + _L0_attn_ref(_layernorm(x, axis=-1), L0_attn_qkv_w, L0_attn_qkv_b, L0_attn_out_w, L0_attn_out_b)
    x = x + _L0_ffn_ref(_layernorm(x, axis=-1), L0_ffn_Wqkv, L0_ffn_q_scale, L0_ffn_k_scale, L0_ffn_Wo, L0_ffn_ln_g, L0_ffn_ln_b, L0_ffn_W1, L0_ffn_b1, L0_ffn_W2, L0_ffn_b2)
    return x

_drawn_inputs = setup_inputs


def setup_inputs(seed=0):
    import zlib

    import numpy as np

    out = dict(_drawn_inputs(seed))
    spreads = {'L0_attn_qkv_b': (0.0, 0.1),
     'L0_attn_out_b': (0.0, 0.1),
     'L0_ffn_q_scale': (1.0, 0.6),
     'L0_ffn_k_scale': (1.0, 0.6),
     'L0_ffn_ln_g': (1.0, 0.6),
     'L0_ffn_ln_b': (0.0, 0.8),
     'L0_ffn_b1': (0.0, 0.8),
     'L0_ffn_b2': (0.0, 0.1)}
    factors = {'L0_ffn_W1': 3.671, 'L0_ffn_W2': 3.612}
    for name, (base, spread) in spreads.items():
        noise = np.random.default_rng([zlib.crc32(name.encode()), seed]).standard_normal(out[name].shape)
        drawn = base * np.exp(spread * noise) if base else spread * noise
        out[name] = jnp.asarray(drawn.astype(out[name].dtype))
    for name, factor in factors.items():
        out[name] = (out[name] * factor).astype(out[name].dtype)
    return out
```

```python
from contextlib import ExitStack

import numpy as np

import concourse.bass as bass
from concourse import mybir

ALU = mybir.AluOpType
ACT = mybir.ActivationFunctionType
AX_X = mybir.AxisListType.X
F32 = mybir.dt.float32
BF16 = mybir.dt.bfloat16

P = 128
BATCH, SEQ, E = 8, 512, 128
HEADS, D = 16, 64
INNER = HEADS * D
PAIRS = HEADS // 2
QTILES = SEQ // P
DEPTH = 6
WINDOW = 32
DIM_INNER = int(E * 4 * 2 / 3)
HCH = -(-DIM_INNER // P)
HROWS = [min(P, DIM_INNER - P * i) for i in range(HCH)]
QK_SCALE = 8.0
EPS = 1e-5
MASKED = -1e30
LN2 = float(np.log(2.0))
NORM_FLOOR = 1e-24
NORM_LIFT = 2.0 ** 20

KT_STEP = P - WINDOW
KTILES = (SEQ - P) // KT_STEP + 1
GROUPS = HEADS // 4
STEPS = GROUPS * KTILES
QK_CHUNKS = 4
V_PER_ITEM = 2 * KTILES
A_STEPS = HEADS * QTILES


def rotary_constants():
    f = np.float32
    half = np.arange(0, D, 2, dtype=f)
    inv_freq = f(1.0) / f(10000.0) ** (half / f(D))
    t = np.arange(SEQ, dtype=f)
    freqs = t[:, None] * inv_freq[None, :]
    base_scale = (half + f(0.4 * D)) / f(1.4 * D)
    power = (t - SEQ // 2) / f(WINDOW // 2)
    scale = base_scale[None, :] ** power[:, None]
    cos, sin = np.cos(freqs), np.sin(freqs)
    inv = f(1.0) / scale
    cos_t = np.stack([cos * scale, cos * inv * f(QK_SCALE)])
    sin_t = np.stack([sin * scale, sin * inv * f(QK_SCALE)])
    return (np.concatenate([cos_t, cos_t], -1).astype(f), np.concatenate([-sin_t, sin_t], -1).astype(f))


def mask_constants():
    d = np.arange(P)[:, None] - np.arange(P)[None, :]
    causal = np.where(d >= 0, 0.0, MASKED).astype(np.float32)
    band = np.where((d >= 0) & (d <= WINDOW), 0.0, MASKED).astype(np.float32)
    return causal, np.tile(band, (1, 4))


def build(nc, T, out, depth=DEPTH):
    with ExitStack() as ctx:
        def sb(name, shape, dt=F32):
            return ctx.enter_context(nc.sbuf_tensor(name, shape, dt))

        def psum(name, shape, dt=F32):
            return ctx.enter_context(nc.psum_tensor(name, shape, dt))

        def sem(name):
            return ctx.enter_context(nc.semaphore(name))

        YB = SEQ + 1
        yT = sb("yT", [P, BATCH * YB])
        w_qkv = sb("w_qkv", [P, 3 * INNER])
        w_out = sb("w_out", [P, PAIRS, E])
        w1 = sb("w1", [P, 2 * DIM_INNER])
        w2 = sb("w2", [P, HCH, E])
        qT = sb("qT", [P, PAIRS, SEQ])
        kE = sb("kE", [P, PAIRS, SEQ])
        kO = sb("kO", [P, PAIRS, SEQ])
        V = sb("V", [P, KTILES, INNER])
        attnT = sb("attnT", [P, PAIRS, SEQ])
        qkn = sb("qkn", [P, 2, 2 * INNER])
        rot_c = sb("rot_c", [P, 2, 512])
        rot_s = sb("rot_s", [P, 2, 512])
        mask_f = rot_c[:].rearrange("p a c -> p (a c)")[:, 0:5 * P]
        sq = sb("sq", [P, 2, 512])
        prob = sb("prob", [P, 2, 512])
        probT = sb("probT", [P, 2, 4, 512])
        base_c = sb("base_c", [P, 2, QTILES, D])
        base_s = sb("base_s", [P, 2, QTILES, D])
        tab_c = sb("tab_c", [P, 2, QTILES, D])
        tab_s = sb("tab_s", [P, 2, QTILES, D])
        scale_d = sb("scale_d", [P, 2, DEPTH * D])
        scale_sw = sb("scale_sw", [P, 2, DEPTH * D])
        identf = sb("identf", [P, P])
        identb = sb("identb", [P, P], BF16)
        causal = sb("causal", [P, P], BF16)
        band = sb("band", [P, 4 * P], BF16)
        mean_w = sb("mean_w", [P, P])
        eps_c = sb("eps_c", [P, 1])
        lift_c = sb("lift_c", [P, 1])
        bq = sb("bq", [P, PAIRS])
        bk = sb("bk", [P, PAIRS])
        bv = sb("bv", [P, PAIRS])
        b_out = sb("b_out", [P, 1])
        ln_gb = sb("ln_gb", [P, 2, DEPTH])
        b1 = sb("b1", [P, 2, HCH, DEPTH])
        b2 = sb("b2", [P, DEPTH])
        xs = sb("xs", [P, SEQ])
        xin = sb("xin", [P, SEQ])
        xc = sb("xc", [P, SEQ])
        rstd = sb("rstd", [P, SEQ])
        xn = sb("xn", [P, SEQ])
        n2 = sb("n2", [P, 2, 2 * HEADS])
        rn = sb("rn", [P, 2, 2 * HEADS])
        nm = sb("nm", [P, 4 * STEPS])
        rs = sb("rs", [P, 4 * STEPS])
        ri = sb("ri", [P, 4 * STEPS])
        x_tok = sb("x_tok", [P, QTILES, E])

        pj = [psum(f"pj{i}", [P, 512]) for i in range(2)]
        pt = [psum(f"pt{i}", [P, 512]) for i in range(2)]
        ps = [psum(f"ps{i}", [P, 512]) for i in range(2)]
        po = [psum(f"po{i}", [P, 512]) for i in range(2)]

        names = """const_in consts w_in wl_in wf_in x_in x_turned xin_ok
            ln_src ln_mean ln_centred ln_squared ln_var ln_log ln_rstd ln_scaled ln_done
            xs_ok qk_mm squared summed rotated added n2_ok rn_log rn_ok qk_ok tqk tqk_out
            v_mm v_out scored maxed exped recipd pnorm pturned pt_out pv_done o_out wo_mm y1
            gate_mm a_mm gelu prod w2_mm y2 tabs
            aq_mm aq_out ak_mm ak_out av_mm av_out a_scored a_maxed a_exped a_recip a_norm a_turned
            a_pt_out a_pv a_o_out a_wo a_x1 a_x1c y0 zeroed fin_add fin_turned fin_out stored x1_stored x1_in""".split()
        S = {k: sem(k) for k in names}

        block = ctx.enter_context(nc.Block())

        @block.sync
        def _(sp):
            with nc.allow_non_contiguous_dma(reason="small vectors, once"):
                sp.dma_start(x_tok[:], T["x"][bass.ds(0, 1)].rearrange("o (t p) e -> p (o t) e", p=P)).then_inc(S["x_in"], 16)
                for j in range(3):
                    sp.dma_start(w_qkv[:, j * INNER:(j + 1) * INNER].rearrange("e (h d) -> e h d", d=D),
                                 T["a_qkv_w"][:, :, j * D:(j + 1) * D]).then_inc(S["w_in"], 16)
                sp.dma_start(w_out[:], T["a_out_w"].rearrange("(c two) d e -> (two d) c e", two=2)).then_inc(S["w_in"], 16)
                c = S["const_in"]
                for r in range(2):
                    sp.dma_start(base_c[:, r], T["rot_c"][r].rearrange("(t p) d -> p t d", p=P)).then_inc(c, 16)
                    sp.dma_start(base_s[:, r], T["rot_s"][r].rearrange("(t p) d -> p t d", p=P)).then_inc(c, 16)
                for r, nme in enumerate(("q_scale", "k_scale")):
                    flat = T[nme].rearrange("l d -> (l d)").unsqueeze(0).to_broadcast([P, DEPTH * D])
                    sp.dma_start(scale_d[:, r], flat).then_inc(c, 16)
                sp.dma_start(identf[:], T["ident"]).then_inc(c, 16)
                sp.dma_start(mask_f, T["masks"]).then_inc(c, 16)
                qkv_b = T["a_qkv_b"].rearrange("(c two) (j d) -> j two d c", two=2, j=3)
                for j, dst in enumerate((bq, bk, bv)):
                    for two in range(2):
                        sp.dma_start(dst[two * D:(two + 1) * D, :], qkv_b[j, two]).then_inc(c, 16)
                sp.dma_start(b_out[:], T["a_out_b"].unsqueeze(1)).then_inc(c, 16)
                sp.dma_start(ln_gb[:, 0], T["ln_g"].rearrange("l e -> e l")).then_inc(c, 16)
                sp.dma_start(ln_gb[:, 1], T["ln_b"].rearrange("l e -> e l")).then_inc(c, 16)
                for ag in range(2):
                    for i in range(HCH):
                        lo = ag * DIM_INNER + i * P
                        sp.dma_start(b1[0:HROWS[i], ag, i], T["b1"][:, lo:lo + HROWS[i]].rearrange("l e -> e l")).then_inc(c, 16)
                sp.dma_start(b2[:], T["b2"].rearrange("l e -> e l")).then_inc(c, 16)
                with sp.Fori(1, BATCH) as b:
                    sp.wait_ge(S["x_turned"], b)
                    sp.dma_start(x_tok[:], T["x"][bass.ds(b, 1)].rearrange("o (t p) e -> p (o t) e", p=P)).then_inc(S["x_in"], 16)
                    sp.wait_ge(S["ln_src"], b * 2)
                    sp.dma_start(T["x1"][bass.ds(b - 1, 1)].rearrange("o e s -> e (o s)"), xin[:]).then_inc(S["x1_stored"], 16)
                sp.wait_ge(S["ln_src"], BATCH * 2)
                sp.dma_start(T["x1"][BATCH - 1], xin[:]).then_inc(S["x1_stored"], 16)
                with sp.Fori(0, depth) as l:
                    sp.wait_ge(S["av_mm"], BATCH * 2 * QTILES)
                    sp.wait_ge(S["v_mm"], l * (BATCH * V_PER_ITEM))
                    sp.dma_start(w_qkv[:], T["Wqkv"][bass.ds(l, 1)].rearrange("o e c -> e (o c)")).then_inc(S["w_in"], 16)
                    sp.wait_ge(S["a_wo"], BATCH)
                    sp.wait_ge(S["w2_mm"], l * BATCH)
                    sp.dma_start(w_out[:], T["Wo"][bass.ds(l, 1)].rearrange("o (c p) e -> p (o c) e", p=P)).then_inc(S["wl_in"], 16)
                    sp.dma_start(w1[:], T["W1"][bass.ds(l, 1)].rearrange("o e c -> e (o c)")).then_inc(S["wl_in"], 16)
                    for i in range(HCH):
                        sp.dma_start(w2[0:HROWS[i], i], T["W2"][bass.ds(l, 1), i * P:i * P + HROWS[i]].rearrange("o p e -> p (o e)")).then_inc(S["wl_in"], 16)
                sp.wait_ge(S["x1_stored"], 16 * BATCH)
                with sp.Fori(0, BATCH) as b:
                    sp.wait_ge(S["y2"], depth * BATCH)
                    sp.wait_ge(S["fin_add"], b)
                    sp.dma_start(xs[:], T["x1"][bass.ds(b, 1)].rearrange("o e s -> e (o s)")).then_inc(S["x1_in"], 16)
                    sp.wait_ge(S["fin_out"], b + 1)
                    sp.dma_start(out[bass.ds(b, 1)].rearrange("o (t p) e -> p (o t) e", p=P), x_tok[:]).then_inc(S["stored"], 16)
                sp.wait_ge(S["stored"], 16 * BATCH)

        @block.tensor
        def _(pe):
            def layernorm(k):
                pe.wait_ge(S["ln_src"], k + 1)
                pe.matmul(pj[1][:], mean_w[:], xin[:], start=True, stop=True).then_inc(S["ln_mean"], 1)
                pe.wait_ge(S["ln_squared"], k + 1)
                pe.matmul(pj[0][:], mean_w[:], sq[:, 0], start=True, stop=True).then_inc(S["ln_var"], 1)

            pe.wait_ge(S["consts"], 1)
            pe.wait_ge(S["w_in"], 64)
            pe.wait_ge(S["zeroed"], 1)
            with pe.Fori(0, BATCH) as b:
                pe.wait_ge(S["x_in"], b * 16 + 16)
                for t in range(QTILES):
                    m = pe.transpose(pt[0][:, t * P:(t + 1) * P], x_tok[:, t], identf[:])
                m.then_inc(S["x_turned"], 1)
                layernorm(b * 2)
                pe.wait_ge(S["ln_done"], b + 1)
                for c in range(PAIRS):
                    if c >= 1:
                        pe.wait_ge(S["aq_out"], b * PAIRS + c)
                    pe.matmul(pj[0][:], w_qkv[:, c * P:(c + 1) * P], xn[:], start=True, stop=True).then_inc(S["aq_mm"], 1)
                    if c >= 1:
                        pe.wait_ge(S["ak_out"], b * PAIRS + c)
                    pe.matmul(pj[1][:], w_qkv[:, INNER + c * P:INNER + (c + 1) * P], xn[:], start=True, stop=True).then_inc(S["ak_mm"], 1)
                for t in range(QTILES):
                    for g in range(2):
                        if t == 0:
                            pe.wait_ge(S["aq_out"], b * PAIRS + PAIRS) if g == 0 else pe.wait_ge(S["ak_out"], b * PAIRS + PAIRS)
                        else:
                            pe.wait_ge(S["av_out"], b * (2 * QTILES) + 2 * t + g - 1)
                        pe.matmul(pj[g][:], xn[:, t * P:(t + 1) * P], w_qkv[:, 2 * INNER + g * 512:2 * INNER + (g + 1) * 512], start=True, stop=True).then_inc(S["av_mm"], 1)

                def score(s):
                    h, qt = divmod(s, QTILES)
                    if s == 0:
                        pe.wait_ge(S["ak_out"], b * PAIRS + PAIRS)
                    if s >= 2:
                        pe.wait_ge(S["a_exped"], b * A_STEPS + s - 1)
                    k = (kE, kO)[h % 2]
                    n = (qt + 1) * P
                    pe.matmul(ps[s % 2][:, n - P:n], identb[:], causal[:], start=True, stop=False, skip_group_check=True)
                    pe.matmul(ps[s % 2][:, 0:n], qT[:, h // 2, qt * P:(qt + 1) * P], k[:, h // 2, 0:n],
                              start=False, stop=True, skip_group_check=True).then_inc(S["a_scored"], 1)

                def turn(s):
                    h, qt = divmod(s, QTILES)
                    pe.wait_ge(S["a_norm"], b * A_STEPS + s + 1)
                    if s >= 2:
                        pe.wait_ge(S["a_pt_out"], b * A_STEPS + s - 1)
                    for kt in range(qt + 1):
                        m = pe.transpose(pt[s % 2][:, kt * P:(kt + 1) * P], prob[:, s % 2, kt * P:(kt + 1) * P], identf[:])
                    m.then_inc(S["a_turned"], 1)

                def weigh(h):
                    c, r = divmod(h, 2)
                    pe.wait_ge(S["a_pt_out"], b * A_STEPS + (h + 1) * QTILES)
                    if h == 0:
                        pe.wait_ge(S["av_out"], b * (2 * QTILES) + 2 * QTILES)
                    if r == 0:
                        if c >= 2:
                            pe.wait_ge(S["a_o_out"], b * PAIRS + c - 1)
                    for kt in range(QTILES):
                        m = pe.matmul(po[c % 2][r * D:(r + 1) * D, kt * P:SEQ], V[:, kt, h * D:(h + 1) * D],
                                      probT[:, h % 2, kt, kt * P:SEQ], start=(kt == 0), stop=(kt == QTILES - 1),
                                      skip_group_check=True)
                    m.then_inc(S["a_pv"], 1)

                for s in range(A_STEPS + 2):
                    if s < A_STEPS:
                        score(s)
                    if 1 <= s <= A_STEPS:
                        turn(s - 1)
                    if s >= 2 and (s - 2) % QTILES == QTILES - 1:
                        weigh((s - 2) // QTILES)
                pe.wait_ge(S["a_o_out"], b * PAIRS + PAIRS)
                for c in range(PAIRS):
                    m = pe.matmul(pj[0][:], w_out[:, c], attnT[:, c], start=(c == 0), stop=(c == PAIRS - 1))
                m.then_inc(S["a_wo"], 1)
                layernorm(b * 2 + 1)

            with pe.Fori(0, depth) as l:
                with pe.Fori(0, BATCH) as b:
                    n = l * BATCH + b
                    pe.wait_ge(S["w_in"], l * 16 + 80)
                    pe.wait_ge(S["wl_in"], l * (16 * (2 + HCH)) + 16 * (2 + HCH))

                    def project_qk(t):
                        if t == 0:
                            pe.wait_ge(S["xs_ok"], n + 1)
                            pe.wait_ge(S["prod"], n * HCH)
                            pe.wait_ge(S["y2"], n)
                        for c in range(QK_CHUNKS):
                            u = t * QK_CHUNKS + c
                            if u >= 2:
                                pe.wait_ge(S["rotated"], n * (QTILES * QK_CHUNKS) + u - 1)
                            pe.matmul(pj[u % 2][:], xs[:, t * P:(t + 1) * P], w_qkv[:, c * 512:(c + 1) * 512],
                                      start=True, stop=True).then_inc(S["qk_mm"], 1)

                    def turn_qk(t):
                        pe.wait_ge(S["qk_ok"], n * QTILES + t + 1)
                        for j in range(QK_CHUNKS):
                            u = t * QK_CHUNKS + j
                            if u >= 2:
                                pe.wait_ge(S["tqk_out"], n * (QTILES * QK_CHUNKS) + u - 1)
                            for i in range(4):
                                m = pe.transpose(pt[j % 2][:, i * P:(i + 1) * P],
                                                 qkn[:, t % 2, (4 * j + i) * P:(4 * j + i + 1) * P], identf[:])
                            m.then_inc(S["tqk"], 1)

                    def project_v(v):
                        kt, g = divmod(v, 2)
                        if v < 2:
                            pe.wait_ge(S["rotated"], n * (QTILES * QK_CHUNKS) + QTILES * QK_CHUNKS - 1 + v)
                        else:
                            pe.wait_ge(S["v_out"], n * V_PER_ITEM + v - 1)
                        lo = 2 * INNER + g * 512
                        pe.matmul(pj[v % 2][:], xs[:, kt * KT_STEP:kt * KT_STEP + P], w_qkv[:, lo:lo + 512],
                                  start=True, stop=True).then_inc(S["v_mm"], 1)

                    def score(s):
                        g, kt = divmod(s, KTILES)
                        if s == 0:
                            pe.wait_ge(S["tqk_out"], n * (QTILES * QK_CHUNKS) + QTILES * QK_CHUNKS)
                        if s >= 2:
                            pe.wait_ge(S["exped"], n * STEPS + s - 1)
                        pe.matmul(ps[s % 2][:], identb[:], band[:], start=True, stop=False, skip_group_check=True)
                        r0 = kt * KT_STEP
                        for i in range(4):
                            h = 4 * g + i
                            k = (kE, kO)[h % 2]
                            m = pe.matmul(ps[s % 2][:, i * P:(i + 1) * P], qT[:, h // 2, r0:r0 + P], k[:, h // 2, r0:r0 + P],
                                          start=False, stop=True, skip_group_check=True)
                        m.then_inc(S["scored"], 1)

                    def turn(s):
                        pe.wait_ge(S["pnorm"], n * STEPS + s + 1)
                        if s >= 2:
                            pe.wait_ge(S["pt_out"], n * STEPS + s - 1)
                        for i in range(4):
                            m = pe.transpose(pt[s % 2][:, i * P:(i + 1) * P], prob[:, s % 2, i * P:(i + 1) * P], identf[:])
                        m.then_inc(S["pturned"], 1)

                    def weigh(s):
                        g, kt = divmod(s, KTILES)
                        pe.wait_ge(S["pt_out"], n * STEPS + s + 1)
                        if s == 0:
                            pe.wait_ge(S["v_out"], n * V_PER_ITEM + V_PER_ITEM)
                        if kt == 0 and g >= 1:
                            pe.wait_ge(S["o_out"], n * PAIRS + 2 * g)
                        c0 = 0 if kt == 0 else WINDOW
                        for i in range(4):
                            h = 4 * g + i
                            m = pe.matmul(po[i // 2][(i % 2) * D:(i % 2 + 1) * D, kt * KT_STEP + c0:kt * KT_STEP + P],
                                          V[:, kt, h * D:(h + 1) * D], probT[:, s % 2, i, c0:P],
                                          start=True, stop=True, skip_group_check=True)
                        m.then_inc(S["pv_done"], 1)

                    for t in range(QTILES + 1):
                        if t < QTILES:
                            project_qk(t)
                        if t >= 1:
                            turn_qk(t - 1)
                    for v in range(V_PER_ITEM):
                        project_v(v)
                    for s in range(STEPS + 2):
                        if s < STEPS:
                            score(s)
                        if 1 <= s <= STEPS:
                            turn(s - 1)
                        if s >= 2:
                            weigh(s - 2)
                    pe.wait_ge(S["o_out"], n * PAIRS + PAIRS)
                    for c in range(PAIRS):
                        m = pe.matmul(pj[0][:], w_out[:, c], attnT[:, c], start=(c == 0), stop=(c == PAIRS - 1))
                    m.then_inc(S["wo_mm"], 1)
                    layernorm(n + 2 * BATCH)
                    pe.wait_ge(S["ln_done"], n + BATCH + 1)
                    for i in range(HCH):
                        M = HROWS[i]
                        if i >= 1:
                            pe.wait_ge(S["gelu"], n * HCH + i)
                        pe.matmul(pj[1][0:M, :], w1[:, DIM_INNER + i * P:DIM_INNER + i * P + M], xn[:],
                                  start=True, stop=True).then_inc(S["gate_mm"], 1)
                        if i >= 1:
                            pe.wait_ge(S["prod"], n * HCH + i)
                        pe.matmul(pj[0][0:M, :], w1[:, i * P:i * P + M], xn[:], start=True, stop=True).then_inc(S["a_mm"], 1)
                    pe.wait_ge(S["prod"], n * HCH + HCH)
                    for i in range(HCH):
                        M = HROWS[i]
                        m = pe.matmul(pj[1][:], w2[0:M, i], probT[0:M, 0, i], start=(i == 0), stop=(i == HCH - 1))
                    m.then_inc(S["w2_mm"], 1)

            with pe.Fori(0, BATCH) as b:
                pe.wait_ge(S["fin_add"], b + 1)
                pe.wait_ge(S["fin_out"], b)
                for t in range(QTILES):
                    m = pe.transpose(pt[0][:, t * P:(t + 1) * P], xin[:, t * P:(t + 1) * P], identf[:])
                m.then_inc(S["fin_turned"], 1)

        @block.vector
        def _(dve):
            def layernorm(k):
                dve.wait_ge(S["ln_mean"], k + 1)
                dve.tensor_tensor(xc[:], xin[:], pj[1][:], ALU.subtract).then_inc(S["ln_centred"], 1)
                dve.wait_ge(S["ln_rstd"], k + 1)

            def shifted(base, dst, done):
                dve.tensor_scalar(dst[0:D, :], yT[0:D, bass.ds(base + 1, SEQ)], 1.0, None, ALU.mult)
                dve.tensor_scalar(dst[D:P, :], yT[D:P, bass.ds(base, SEQ)], 1.0, None, ALU.mult).then_inc(done, 1)

            dve.memset(kE[D:P], 0.0)
            dve.memset(kO[0:D], 0.0)
            dve.memset(mean_w[:], 1.0 / E)
            dve.memset(eps_c[:], EPS)
            dve.memset(lift_c[:], 0.5 * np.log(NORM_LIFT).item())
            dve.memset(yT[:], 0.0).then_inc(S["zeroed"], 1)
            dve.wait_ge(S["const_in"], 16 * N_CONST)
            dve.tensor_copy(identb[:], identf[:])
            dve.tensor_copy(causal[:], mask_f[:, 0:P])
            dve.tensor_scalar(bq[:], bq[:], 1.0 / 8.0, None, ALU.mult)
            for r in range(2):
                v = scale_d[:, r].rearrange("p (l s j) -> p l s j", s=2, j=D // 2)
                dve.tensor_copy(scale_sw[:, r].rearrange("p (l s j) -> p l s j", s=2, j=D // 2), v[:, :, ::-1, :])
            dve.tensor_copy(band[:], mask_f[:, P:5 * P]).then_inc(S["consts"], 1)

            with dve.Fori(0, BATCH) as b:
                dve.wait_ge(S["x_turned"], b + 1)
                dve.wait_ge(S["x1_stored"], b * 16)
                dve.tensor_copy(xin[:], pt[0][:]).then_inc(S["ln_src"], 1)
                dve.wait_ge(S["ln_src"], b * 2 + 1)
                layernorm(b * 2)
                dve.tensor_tensor(xn[:], xc[:], rstd[:], ALU.mult).then_inc(S["ln_done"], 1)
                for s in range(A_STEPS + 2):
                    if s < A_STEPS:
                        n = (s % QTILES + 1) * P
                        dve.wait_ge(S["a_scored"], b * A_STEPS + s + 1)
                        dve.tensor_reduce(nm[:, s:s + 1], ps[s % 2][:, 0:n], AX_X, ALU.max, negate=True).then_inc(S["a_maxed"], 1)
                    if 1 <= s <= A_STEPS:
                        k = s - 1
                        n = (k % QTILES + 1) * P
                        dve.wait_ge(S["a_exped"], b * A_STEPS + k + 1)
                        dve.reciprocal(ri[:, k:k + 1], rs[:, k:k + 1]).then_inc(S["a_recip"], 1)
                        dve.wait_ge(S["a_recip"], b * A_STEPS + k + 1)
                        dve.tensor_scalar(prob[:, k % 2, 0:n], prob[:, k % 2, 0:n], ri[:, k:k + 1], None, ALU.mult).then_inc(S["a_norm"], 1)
                    if s >= 2:
                        k = s - 2
                        h, qt = divmod(k, QTILES)
                        dve.wait_ge(S["a_turned"], b * A_STEPS + k + 1)
                        if h >= 2 and qt == 0:
                            dve.wait_ge(S["a_pv"], b * HEADS + h - 1)
                        n = (qt + 1) * P
                        dve.tensor_copy(probT[:, h % 2, 0:qt + 1, qt * P:(qt + 1) * P],
                                        pt[k % 2][:, 0:n].rearrange("p (k q) -> p k q", q=P)).then_inc(S["a_pt_out"], 1)
                dve.wait_ge(S["a_wo"], b + 1)
                dve.scalar_tensor_tensor(out=xin[:], in0=pj[0][:], scalar=b_out[:, 0:1], in1=xin[:], op0=ALU.add, op1=ALU.add).then_inc(S["ln_src"], 1)
                dve.wait_ge(S["ln_src"], b * 2 + 2)
                layernorm(b * 2 + 1)
                dve.tensor_tensor(yT[:, bass.ds(b * YB + 1, SEQ)], xc[:], rstd[:], ALU.mult).then_inc(S["y0"], 1)

            dve.wait_ge(S["y0"], BATCH)
            with dve.Fori(0, depth) as l:
                dve.wait_ge(S["rotated"], l * (BATCH * QTILES * QK_CHUNKS))
                for r in range(2):
                    sd = scale_d[:, r, bass.ds(l * D, D)].unsqueeze(1).to_broadcast([P, QTILES, D])
                    ss = scale_sw[:, r, bass.ds(l * D, D)].unsqueeze(1).to_broadcast([P, QTILES, D])
                    dve.tensor_tensor(tab_c[:, r], base_c[:, r], sd, ALU.mult)
                    dve.tensor_tensor(tab_s[:, r], base_s[:, r], ss, ALU.mult).then_inc(S["tabs"], 1)
                with dve.Fori(0, BATCH) as b:
                    n = l * BATCH + b
                    dve.wait_ge(S["tabs"], l * 2 + 2)
                    dve.wait_ge(S["v_mm"], n * V_PER_ITEM)
                    dve.wait_ge(S["y2"], n)
                    shifted(b * YB, xs, S["xs_ok"])

                    def rotate(t):
                        for c in range(QK_CHUNKS):
                            u = t * QK_CHUNKS + c
                            r = c // 2
                            dve.wait_ge(S["squared"], n * (QTILES * QK_CHUNKS) + u + 1)
                            dve.tensor_reduce(n2[:, t % 2, 8 * c:8 * c + 8], sq[:, u % 2].rearrange("p (h d) -> p h d", d=D),
                                              AX_X, ALU.add).then_inc(S["summed"], 1)
                            if u >= 2:
                                dve.wait_ge(S["added"], n * (QTILES * QK_CHUNKS) + u - 1)
                            elif u == 0:
                                dve.wait_ge(S["added"], n * (QTILES * QK_CHUNKS))
                            heads = pj[u % 2][:].rearrange("p (h d) -> p h d", d=D)
                            swapped = pj[u % 2][:].rearrange("p (h s j) -> p h s j", s=2, j=D // 2)[:, :, ::-1, :]
                            tc = tab_c[:, r, t].unsqueeze(1).to_broadcast([P, 8, D])
                            ts = tab_s[:, r, t].rearrange("p (s j) -> p s j", s=2).unsqueeze(1).to_broadcast([P, 8, 2, D // 2])
                            dve.tensor_tensor(rot_c[:, u % 2].rearrange("p (h d) -> p h d", d=D), heads, tc, ALU.mult)
                            dve.tensor_tensor(rot_s[:, u % 2].rearrange("p (h s j) -> p h s j", s=2, j=D // 2),
                                              swapped, ts, ALU.mult).then_inc(S["rotated"], 1)
                        dve.wait_ge(S["summed"], n * (QTILES * QK_CHUNKS) + (t + 1) * QK_CHUNKS)
                        dve.tensor_scalar(n2[:, t % 2], n2[:, t % 2], NORM_FLOOR, None, ALU.max).then_inc(S["n2_ok"], 1)

                    def normalise(t):
                        dve.wait_ge(S["rn_ok"], n * QTILES + t + 1)
                        dve.wait_ge(S["added"], n * (QTILES * QK_CHUNKS) + (t + 1) * QK_CHUNKS)
                        v = qkn[:, t % 2].rearrange("p (h d) -> p h d", d=D)
                        dve.tensor_tensor(v, v, rn[:, t % 2].unsqueeze(2).to_broadcast([P, 2 * HEADS, D]), ALU.mult).then_inc(S["qk_ok"], 1)

                    for t in range(QTILES + 1):
                        if t < QTILES:
                            rotate(t)
                        if t >= 1:
                            normalise(t - 1)
                    for s in range(STEPS + 2):
                        if s < STEPS:
                            dve.wait_ge(S["scored"], n * STEPS + s + 1)
                            dve.tensor_reduce(nm[:, 4 * s:4 * s + 4], ps[s % 2][:].rearrange("p (h k) -> p h k", h=4),
                                              AX_X, ALU.max, negate=True).then_inc(S["maxed"], 1)
                        if 1 <= s <= STEPS:
                            k = s - 1
                            dve.wait_ge(S["exped"], n * STEPS + k + 1)
                            dve.reciprocal(ri[:, 4 * k:4 * k + 4], rs[:, 4 * k:4 * k + 4]).then_inc(S["recipd"], 1)
                        if s >= 2:
                            k = s - 2
                            dve.wait_ge(S["pturned"], n * STEPS + k + 1)
                            if k >= 2:
                                dve.wait_ge(S["pv_done"], n * STEPS + k - 1)
                            elif k == 0:
                                dve.wait_ge(S["w2_mm"], n)
                            dve.tensor_copy(probT[:, k % 2, :, 0:P], pt[k % 2][:].rearrange("p (h q) -> p h q", h=4)).then_inc(S["pt_out"], 1)
                    dve.wait_ge(S["wo_mm"], n + 1)
                    y = yT[:, bass.ds(b * YB + 1, SEQ)]
                    dve.tensor_tensor(y, y, pj[0][:], ALU.add).then_inc(S["y1"], 1)
                    dve.wait_ge(S["y1"], n + 1)
                    shifted(b * YB, xin, S["ln_src"])
                    dve.wait_ge(S["ln_src"], n + 2 * BATCH + 1)
                    layernorm(n + 2 * BATCH)
                    dve.tensor_tensor(xn[:], xc[:], rstd[:], ALU.mult).then_inc(S["ln_scaled"], 1)
                    dve.wait_ge(S["ln_scaled"], n + 1)
                    dve.tensor_scalar(xn[:], xn[:], ln_gb[:, 0, bass.ds(l, 1)], ln_gb[:, 1, bass.ds(l, 1)], ALU.mult, ALU.add).then_inc(S["ln_done"], 1)
                    for i in range(HCH):
                        M = HROWS[i]
                        dve.wait_ge(S["gelu"], n * HCH + i + 1)
                        dve.wait_ge(S["a_mm"], n * HCH + i + 1)
                        dve.scalar_tensor_tensor(out=probT[0:M, 0, i], in0=pj[0][0:M, :], scalar=b1[0:M, 0, i, bass.ds(l, 1)],
                                                 in1=probT[0:M, 1, i], op0=ALU.add, op1=ALU.mult).then_inc(S["prod"], 1)
                    dve.wait_ge(S["w2_mm"], n + 1)
                    dve.scalar_tensor_tensor(out=y, in0=pj[1][:], scalar=b2[:, bass.ds(l, 1)], in1=y, op0=ALU.add, op1=ALU.add).then_inc(S["y2"], 1)

            dve.wait_ge(S["y2"], depth * BATCH)
            with dve.Fori(0, BATCH) as b:
                dve.wait_ge(S["fin_turned"], b)
                dve.wait_ge(S["x1_in"], b * 16 + 16)
                dve.tensor_tensor(xin[:], xs[:], yT[:, bass.ds(b * YB + 1, SEQ)], ALU.add).then_inc(S["fin_add"], 1)

        @block.scalar
        def _(act):
            def layernorm(k):
                act.wait_ge(S["ln_centred"], k + 1)
                act.activation(sq[:, 0], xc[:], ACT.Square).then_inc(S["ln_squared"], 1)
                act.wait_ge(S["ln_var"], k + 1)
                act.activation(rstd[:], pj[0][:], ACT.Ln, bias=eps_c[:, 0:1]).then_inc(S["ln_log"], 1)
                act.wait_ge(S["ln_log"], k + 1)
                act.activation(rstd[:], rstd[:], ACT.Exp, scale=-0.5).then_inc(S["ln_rstd"], 1)

            act.preload_act_table_set("natural_log_exp_and_others")
            act.wait_ge(S["zeroed"], 1)
            act.wait_ge(S["consts"], 1)
            with act.Fori(0, BATCH) as b:
                layernorm(b * 2)
                for c in range(PAIRS):
                    act.wait_ge(S["aq_mm"], b * PAIRS + c + 1)
                    act.activation(qT[:, c], pj[0][:], ACT.Identity, bias=bq[:, c:c + 1], scale=1.0 / 8.0).then_inc(S["aq_out"], 1)
                    act.wait_ge(S["ak_mm"], b * PAIRS + c + 1)
                    act.activation(kE[0:D, c], pj[1][0:D, :], ACT.Identity, bias=bk[0:D, c:c + 1])
                    act.activation(kO[D:P, c], pj[1][D:P, :], ACT.Identity, bias=bk[D:P, c:c + 1]).then_inc(S["ak_out"], 1)
                for t in range(QTILES):
                    for g in range(2):
                        act.wait_ge(S["av_mm"], b * (2 * QTILES) + 2 * t + g + 1)
                        act.activation(V[:, t, g * 512:(g + 1) * 512], pj[g][:], ACT.Copy).then_inc(S["av_out"], 1)
                for s in range(A_STEPS + 3):
                    if s < A_STEPS:
                        n = (s % QTILES + 1) * P
                        act.wait_ge(S["a_maxed"], b * A_STEPS + s + 1)
                        if s >= 2:
                            act.wait_ge(S["a_turned"], b * A_STEPS + s - 1)
                        act.activation(prob[:, s % 2, 0:n], ps[s % 2][:, 0:n], ACT.Exp, bias=nm[:, s:s + 1],
                                       accum_out=rs[:, s:s + 1]).then_inc(S["a_exped"], 1)
                    if s >= 3 and (s - 3) % (2 * QTILES) == 2 * QTILES - 1:
                        c = (s - 3) // (2 * QTILES)
                        act.wait_ge(S["a_pv"], b * HEADS + 2 * c + 2)
                        act.activation(attnT[:, c], po[c % 2][:], ACT.Identity, bias=bv[:, c:c + 1]).then_inc(S["a_o_out"], 1)
                layernorm(b * 2 + 1)

            with act.Fori(0, depth) as l:
                with act.Fori(0, BATCH) as b:
                    n = l * BATCH + b

                    def square(t):
                        for c in range(QK_CHUNKS):
                            u = t * QK_CHUNKS + c
                            act.wait_ge(S["qk_mm"], n * (QTILES * QK_CHUNKS) + u + 1)
                            if u >= 2:
                                act.wait_ge(S["summed"], n * (QTILES * QK_CHUNKS) + u - 1)
                            act.activation(sq[:, u % 2], pj[u % 2][:], ACT.Square).then_inc(S["squared"], 1)

                    def inverse_norm(t):
                        act.wait_ge(S["n2_ok"], n * QTILES + t + 1)
                        act.activation(rn[:, t % 2], n2[:, t % 2], ACT.Ln, scale=NORM_LIFT).then_inc(S["rn_log"], 1)
                        act.wait_ge(S["rn_log"], n * QTILES + t + 1)
                        act.activation(rn[:, t % 2], rn[:, t % 2], ACT.Exp, scale=-0.5, bias=lift_c[:, 0:1]).then_inc(S["rn_ok"], 1)

                    def copy_qk(t):
                        cols = slice(t * P, (t + 1) * P)
                        for j in range(QK_CHUNKS):
                            act.wait_ge(S["tqk"], n * (QTILES * QK_CHUNKS) + t * QK_CHUNKS + j + 1)
                            src = pt[j % 2][:].rearrange("p (c q) -> p c q", c=4)
                            pair = slice(4 * (j % 2), 4 * (j % 2) + 4)
                            if j < 2:
                                act.activation(qT[:, pair, cols], src, ACT.Copy).then_inc(S["tqk_out"], 1)
                            else:
                                act.activation(kE[0:D, pair, cols], src[0:D], ACT.Copy)
                                act.activation(kO[D:P, pair, cols], src[D:P], ACT.Copy).then_inc(S["tqk_out"], 1)

                    for t in range(QTILES + 1):
                        if t < QTILES:
                            square(t)
                            inverse_norm(t)
                        if t >= 1:
                            copy_qk(t - 1)
                    for v in range(V_PER_ITEM):
                        kt, g = divmod(v, 2)
                        act.wait_ge(S["v_mm"], n * V_PER_ITEM + v + 1)
                        act.activation(V[:, kt, g * 512:(g + 1) * 512], pj[v % 2][:], ACT.Copy).then_inc(S["v_out"], 1)
                    for s in range(STEPS + 3):
                        if s < STEPS:
                            act.wait_ge(S["maxed"], n * STEPS + s + 1)
                            if s >= 2:
                                act.wait_ge(S["pturned"], n * STEPS + s - 1)
                            for i in range(4):
                                m = act.activation(prob[:, s % 2, i * P:(i + 1) * P], ps[s % 2][:, i * P:(i + 1) * P], ACT.Exp,
                                                   bias=nm[:, 4 * s + i:4 * s + i + 1], accum_out=rs[:, 4 * s + i:4 * s + i + 1])
                            m.then_inc(S["exped"], 1)
                        if s >= 3 and (s - 3) % KTILES == KTILES - 1:
                            g = (s - 3) // KTILES
                            act.wait_ge(S["pv_done"], n * STEPS + s - 2)
                            for i in range(2):
                                act.activation(attnT[:, 2 * g + i], po[i][:], ACT.Copy).then_inc(S["o_out"], 1)
                    layernorm(n + 2 * BATCH)
                    for i in range(HCH):
                        M = HROWS[i]
                        act.wait_ge(S["gate_mm"], n * HCH + i + 1)
                        act.activation(probT[0:M, 1, i], pj[1][0:M, :], ACT.Gelu, bias=b1[0:M, 1, i, bass.ds(l, 1)]).then_inc(S["gelu"], 1)
                    act.preload_act_table_set("natural_log_exp_and_others")

            with act.Fori(0, BATCH) as b:
                act.wait_ge(S["fin_turned"], b + 1)
                act.wait_ge(S["stored"], b * 16)
                act.activation(x_tok[:], pt[0][:].rearrange("p (t e) -> p t e", e=E), ACT.Copy).then_inc(S["fin_out"], 1)

        @block.gpsimd
        def _(pool):
            with pool.Fori(0, depth * BATCH) as n:
                def add(t):
                    for c in range(QK_CHUNKS):
                        u = t * QK_CHUNKS + c
                        pool.wait_ge(S["rotated"], n * (QTILES * QK_CHUNKS) + u + 1)
                        if t >= 2 and c == 0:
                            pool.wait_ge(S["tqk"], n * (QTILES * QK_CHUNKS) + (t - 1) * QK_CHUNKS)
                        if t < 2 and c == 0:
                            pool.wait_ge(S["tqk"], n * (QTILES * QK_CHUNKS))
                        pool.tensor_tensor(qkn[:, t % 2, c * 512:(c + 1) * 512], rot_c[:, u % 2], rot_s[:, u % 2], ALU.add).then_inc(S["added"], 1)

                for t in range(QTILES):
                    add(t)
                for s in range(STEPS):
                    pool.wait_ge(S["recipd"], n * STEPS + s + 1)
                    v = prob[:, s % 2].rearrange("p (h k) -> p h k", h=4)
                    pool.tensor_tensor(v, v, ri[:, 4 * s:4 * s + 4].unsqueeze(2).to_broadcast([P, 4, P]), ALU.mult).then_inc(S["pnorm"], 1)


N_CONST = 4 + 2 + 2 + 6 + 1 + 2 + 2 * HCH + 1


_INS = {'x': 'L0_attn_x', 'a_qkv_w': 'L0_attn_qkv_w', 'a_qkv_b': 'L0_attn_qkv_b', 'a_out_w': 'L0_attn_out_w',
        'a_out_b': 'L0_attn_out_b', 'Wqkv': 'L0_ffn_Wqkv', 'q_scale': 'L0_ffn_q_scale', 'k_scale': 'L0_ffn_k_scale',
        'Wo': 'L0_ffn_Wo', 'ln_g': 'L0_ffn_ln_g', 'ln_b': 'L0_ffn_ln_b', 'W1': 'L0_ffn_W1', 'b1': 'L0_ffn_b1',
        'W2': 'L0_ffn_W2', 'b2': 'L0_ffn_b2'}


def kernel(**inputs):
    import concourse.bacc as _bacc
    from concourse.bass_utils import run_bass_kernel_spmd as _run

    nc = _bacc.Bacc("TRN2", target_bir_lowering=False, num_devices=1)
    arrays, T = {}, {}

    def give(name, a):
        a = np.ascontiguousarray(a)
        arrays[f"in_{name}"] = a
        T[name] = nc.dram_tensor(f"in_{name}", a.shape, mybir.dt.from_np(a.dtype), kind="ExternalInput").ap()

    for name, full in _INS.items():
        give(name, inputs[full])
    rot_c, rot_s = rotary_constants()
    causal, band = mask_constants()
    give("rot_c", rot_c)
    give("rot_s", rot_s)
    give("masks", np.concatenate([causal, band], 1))
    give("ident", np.eye(P, dtype=np.float32))
    T["x1"] = nc.dram_tensor("x1", (BATCH, E, SEQ), F32, kind="Internal").ap()
    out = nc.dram_tensor("out_0", (BATCH, SEQ, E), F32, kind="ExternalOutput").ap()
    build(nc, T, out)
    return _run(nc, [arrays], core_ids=[0]).results[0]["out_0"]
```

```python
from contextlib import ExitStack

import numpy as np

import concourse.bass as bass
from concourse import mybir

ALU = mybir.AluOpType
ACT = mybir.ActivationFunctionType
AX_X = mybir.AxisListType.X
F32 = mybir.dt.float32
BF16 = mybir.dt.bfloat16

P = 128
BATCH, SEQ, E = 8, 512, 128
HEADS, D = 16, 64
INNER = HEADS * D
PAIRS = HEADS // 2
QTILES = SEQ // P
DEPTH = 6
WINDOW = 32
DIM_INNER = int(E * 4 * 2 / 3)
HCH = -(-DIM_INNER // P)
HROWS = [min(P, DIM_INNER - P * i) for i in range(HCH)]
QK_SCALE = 8.0
EPS = 1e-5
MASKED = -1e30
LN2 = float(np.log(2.0))
NORM_FLOOR = 1e-24
NORM_LIFT = 2.0 ** 20

KT_STEP = P - WINDOW
KTILES = (SEQ - P) // KT_STEP + 1
GROUPS = HEADS // 4
STEPS = GROUPS * KTILES
QK_CHUNKS = 4
QK_PER_ITEM = QTILES * QK_CHUNKS
V_PER_ITEM = 2 * KTILES
O_PER_ITEM = 2 * KTILES
A_STEPS = HEADS * QTILES


def rotary_constants():
    f = np.float32
    half = np.arange(0, D, 2, dtype=f)
    inv_freq = f(1.0) / f(10000.0) ** (half / f(D))
    t = np.arange(SEQ, dtype=f)
    freqs = t[:, None] * inv_freq[None, :]
    base_scale = (half + f(0.4 * D)) / f(1.4 * D)
    power = (t - SEQ // 2) / f(WINDOW // 2)
    scale = base_scale[None, :] ** power[:, None]
    cos, sin = np.cos(freqs), np.sin(freqs)
    inv = f(1.0) / scale
    cos_t = np.stack([cos * scale, cos * inv * f(QK_SCALE)])
    sin_t = np.stack([sin * scale, sin * inv * f(QK_SCALE)])
    return (np.concatenate([cos_t, cos_t], -1).astype(f), np.concatenate([-sin_t, sin_t], -1).astype(f))


def mask_constants():
    d = np.arange(P)[:, None] - np.arange(P)[None, :]
    causal = np.where(d >= 0, 0.0, MASKED).astype(np.float32)
    band = np.where((d >= 0) & (d <= WINDOW), 0.0, MASKED).astype(np.float32)
    return causal, np.tile(band, (1, 4))


N_CONST = 4 + 2 + 2 + 6 + 1 + 2 + 2 * HCH + 1
WL_DMAS = 16 * (2 + HCH)


def build(nc, T, out, depth=DEPTH):
    ITEMS = depth * BATCH
    with ExitStack() as ctx:
        def sb(name, shape, dt=F32):
            return ctx.enter_context(nc.sbuf_tensor(name, shape, dt))

        def psum(name):
            return ctx.enter_context(nc.psum_tensor(name, [P, 512], F32))

        def sem(name):
            return ctx.enter_context(nc.semaphore(name))

        YB = SEQ + 1
        yT = sb("yT", [P, BATCH * YB])
        w_qkv = sb("w_qkv", [P, 2, 3 * INNER])
        w_out = sb("w_out", [P, PAIRS, E])
        w1 = sb("w1", [P, 2 * DIM_INNER])
        w2 = sb("w2", [P, HCH, E])
        qT = sb("qT", [P, PAIRS, SEQ])
        kT = sb("kT", [P, PAIRS, SEQ])
        V = sb("V", [P, KTILES, INNER])
        attnT = sb("attnT", [P, PAIRS, SEQ])
        qkn = sb("qkn", [P, 2, 2 * INNER])
        probT_a = qkn[:].rearrange("p a (k q) -> p a k q", q=SEQ)
        rot_c = sb("rot_c", [P, 2, 512])
        rot_s = sb("rot_s", [P, 2, 512])
        mask_f = rot_c[:].rearrange("p a c -> p (a c)")[:, 0:5 * P]
        sq = sb("sq", [P, 2, 512])
        prob = sb("prob", [P, 4, 512])
        probT = sb("probT", [P, 2, 4, P])
        hidden = sb("hidden", [P, HCH, SEQ])
        start = attnT[:].rearrange("p c q -> p (c q)")
        base_c = start[:, 0:512].rearrange("p (r t d) -> p r t d", r=2, t=QTILES)
        base_s = start[:, 512:1024].rearrange("p (r t d) -> p r t d", r=2, t=QTILES)
        scale_d = start[:, 1024:1024 + 2 * DEPTH * D].rearrange("p (r c) -> p r c", r=2)
        scale_sw = start[:, 2048:2048 + 2 * DEPTH * D].rearrange("p (r c) -> p r c", r=2)
        tab_c = sb("tab_c", [P, DEPTH, 2, QTILES, D])
        tab_s = sb("tab_s", [P, DEPTH, 2, QTILES, D])
        identf = sb("identf", [P, P])
        identb = sb("identb", [P, P], BF16)
        causal = sb("causal", [P, P], BF16)
        band = sb("band", [P, 4 * P], BF16)
        mean_w = sb("mean_w", [P, P])
        eps_c = sb("eps_c", [P, 1])
        lift_c = sb("lift_c", [P, 1])
        bq = sb("bq", [P, PAIRS])
        bk = sb("bk", [P, PAIRS])
        bv = sb("bv", [P, PAIRS])
        b_out = sb("b_out", [P, 1])
        ln_gb = sb("ln_gb", [P, 2, DEPTH])
        b1 = sb("b1", [P, 2, HCH, DEPTH])
        b2 = sb("b2", [P, DEPTH])
        xs = sb("xs", [P, SEQ])
        xin = sb("xin", [P, SEQ])
        xn = sb("xn", [P, SEQ])
        rstd = sb("rstd", [P, SEQ])
        n2 = sb("n2", [P, 2, 2 * HEADS])
        rn = sb("rn", [P, 2, 2 * HEADS])
        nm = sb("nm", [P, 4 * STEPS])
        rs = sb("rs", [P, 4 * STEPS])
        ri = sb("ri", [P, 4 * STEPS])
        x_tok = sb("x_tok", [P, QTILES, E])

        pj = [psum(f"pj{i}") for i in range(2)]
        pt = psum("pt")
        px = psum("px")
        ps = [psum(f"ps{i}") for i in range(2)]
        po = [psum(f"po{i}") for i in range(2)]
        pturn = [pt, px]

        names = """const_in consts wa_in wq_in wl_in x_in x_turned x1_stored x1_in zeroed
            ln_src ln_mean ln_centred ln_squared ln_var ln_log ln_rstd ln_scaled ln_done
            xs_ok qk_mm squared summed rotated added n2_ok rn_log rn_ok qk_ok tqk tqk_out
            v_mm v_out scored maxed exped recipd pnorm pturned pt_out pv_done o_out wo_mm y1
            gate_mm gate_out a_mm gelu prod w2_mm y2 tabs
            aq_mm aq_out ak_mm ak_out av_mm av_out a_scored a_maxed a_exped a_recip a_norm a_turned
            a_pt_even a_pt_odd a_pv a_o_out a_wo y0 fin_add fin_turned fin_out stored""".split()
        S = {k: sem(k) for k in names}

        block = ctx.enter_context(nc.Block())

        def first(n):
            return isinstance(n, int) and n == 0

        def second(n):
            return isinstance(n, int) and n == 1

        def at(n, i):
            return (n, i) if i >= 0 else (n - 1, i + STEPS)

        @block.sync
        def _(sp):
            with nc.allow_non_contiguous_dma(reason="small vectors, once"):
                sp.dma_start(x_tok[:], T["x"][0].rearrange("(t p) e -> p t e", p=P)).then_inc(S["x_in"], 16)
                c = S["const_in"]
                sp.dma_start(identf[:], T["ident"]).then_inc(c, 16)
                sp.dma_start(mask_f, T["masks"]).then_inc(c, 16)
                for j in range(3):
                    sp.dma_start(w_qkv[:, 0, j * INNER:(j + 1) * INNER].rearrange("e (h d) -> e h d", d=D),
                                 T["a_qkv_w"][:, :, j * D:(j + 1) * D]).then_inc(S["wa_in"], 16)
                sp.dma_start(w_out[:], T["a_out_w"].rearrange("(c two) d e -> (two d) c e", two=2)).then_inc(S["wa_in"], 16)
                qkv_b = T["a_qkv_b"].rearrange("(c two) (j d) -> j two d c", two=2, j=3)
                for j, dst in enumerate((bq, bk, bv)):
                    for two in range(2):
                        sp.dma_start(dst[two * D:(two + 1) * D, :], qkv_b[j, two]).then_inc(c, 16)
                sp.dma_start(b_out[:], T["a_out_b"].unsqueeze(1)).then_inc(c, 16)
                for r in range(2):
                    sp.dma_start(base_c[:, r], T["rot_c"][r].rearrange("(t p) d -> p t d", p=P)).then_inc(c, 16)
                    sp.dma_start(base_s[:, r], T["rot_s"][r].rearrange("(t p) d -> p t d", p=P)).then_inc(c, 16)
                for r, name in enumerate(("q_scale", "k_scale")):
                    flat = T[name].rearrange("l d -> (l d)").unsqueeze(0).to_broadcast([P, DEPTH * D])
                    sp.dma_start(scale_d[:, r], flat).then_inc(c, 16)
                sp.dma_start(ln_gb[:, 0], T["ln_g"].rearrange("l e -> e l")).then_inc(c, 16)
                sp.dma_start(ln_gb[:, 1], T["ln_b"].rearrange("l e -> e l")).then_inc(c, 16)
                for ag in range(2):
                    for i in range(HCH):
                        lo = ag * DIM_INNER + i * P
                        sp.dma_start(b1[0:HROWS[i], ag, i], T["b1"][:, lo:lo + HROWS[i]].rearrange("l e -> e l")).then_inc(c, 16)
                sp.dma_start(b2[:], T["b2"].rearrange("l e -> e l")).then_inc(c, 16)
                sp.dma_start(w_qkv[:, 1], T["Wqkv"][0]).then_inc(S["wq_in"], 16)
                with sp.Fori(1, BATCH) as b:
                    sp.wait_ge(S["x_turned"], b)
                    sp.dma_start(x_tok[:], T["x"][bass.ds(b, 1)].rearrange("o (t p) e -> p (o t) e", p=P)).then_inc(S["x_in"], 16)
                    sp.wait_ge(S["ln_src"], b * 2)
                    sp.dma_start(T["x1"][bass.ds(b - 1, 1)].rearrange("o e s -> e (o s)"), xin[:]).then_inc(S["x1_stored"], 16)
                sp.wait_ge(S["ln_src"], BATCH * 2)
                sp.dma_start(T["x1"][BATCH - 1], xin[:]).then_inc(S["x1_stored"], 16)

                def load_rest(l):
                    sp.dma_start(w_out[:], T["Wo"][bass.ds(l, 1)].rearrange("o (c p) e -> p (o c) e", p=P)).then_inc(S["wl_in"], 16)
                    sp.dma_start(w1[:], T["W1"][bass.ds(l, 1)].rearrange("o e c -> e (o c)")).then_inc(S["wl_in"], 16)
                    for i in range(HCH):
                        sp.dma_start(w2[0:HROWS[i], i], T["W2"][bass.ds(l, 1), i * P:i * P + HROWS[i]].rearrange("o p e -> p (o e)")).then_inc(S["wl_in"], 16)

                sp.wait_ge(S["a_wo"], BATCH)
                load_rest(0)
                if depth > 1:
                    sp.wait_ge(S["qk_mm"], 1)
                    sp.dma_start(w_qkv[:, 0], T["Wqkv"][1]).then_inc(S["wq_in"], 16)
                if depth > 2:
                    with sp.Fori(1, depth - 1) as l:
                        sp.wait_ge(S["qk_mm"], l * (BATCH * QK_PER_ITEM) + 1)
                        sp.dma_start(w_qkv[:, bass.ds(l % 2, 1)], T["Wqkv"][bass.ds(l + 1, 1)].rearrange("o e c -> e o c")).then_inc(S["wq_in"], 16)
                        sp.wait_ge(S["w2_mm"], l * BATCH)
                        load_rest(l)
                if depth > 1:
                    sp.wait_ge(S["w2_mm"], (depth - 1) * BATCH)
                    load_rest(depth - 1)
                sp.wait_ge(S["x1_stored"], 16 * BATCH + 16)
                sp.wait_ge(S["y2"], ITEMS)
                sp.dma_start(xs[:], T["x1"][0]).then_inc(S["x1_in"], 16)
                with sp.Fori(1, BATCH) as b:
                    sp.wait_ge(S["fin_add"], b)
                    sp.dma_start(xs[:], T["x1"][bass.ds(b, 1)].rearrange("o e s -> e (o s)")).then_inc(S["x1_in"], 16)
                    sp.wait_ge(S["fin_out"], b)
                    sp.dma_start(out[bass.ds(b - 1, 1)].rearrange("o (t p) e -> p (o t) e", p=P), x_tok[:]).then_inc(S["stored"], 16)
                sp.wait_ge(S["fin_out"], BATCH)
                sp.dma_start(out[BATCH - 1].rearrange("(t p) e -> p t e", p=P), x_tok[:]).then_inc(S["stored"], 16)
                sp.wait_ge(S["stored"], 16 * BATCH)

        @block.tensor
        def _(pe):
            def mean(bank, k):
                pe.wait_ge(S["ln_src"], k + 1)
                pe.matmul(bank[:], mean_w[:], xin[:], start=True, stop=True).then_inc(S["ln_mean"], 1)

            def variance(bank, k):
                pe.wait_ge(S["ln_squared"], k + 1)
                pe.matmul(bank[:], mean_w[:], rstd[:], start=True, stop=True).then_inc(S["ln_var"], 1)

            pe.wait_ge(S["consts"], 1)
            pe.wait_ge(S["wa_in"], 64)
            pe.wait_ge(S["zeroed"], 1)
            with pe.Fori(0, BATCH) as b:
                pe.wait_ge(S["x_in"], b * 16 + 16)
                for t in range(QTILES):
                    m = pe.transpose(px[:, t * P:(t + 1) * P], x_tok[:, t], identf[:])
                m.then_inc(S["x_turned"], 1)
                mean(pj[1], b * 2)
                variance(pj[0], b * 2)
                pe.wait_ge(S["ln_done"], b + 1)

                def project_qk(c):
                    if c == 1:
                        pe.wait_ge(S["av_out"], b * (2 * QTILES) + 2 * QTILES)
                    elif c >= 2:
                        pe.wait_ge(S["aq_out"], b * PAIRS + c)
                    pe.matmul(pj[0][:], w_qkv[:, 0, c * P:(c + 1) * P], xn[:], start=True, stop=True).then_inc(S["aq_mm"], 1)
                    if c >= 2:
                        pe.wait_ge(S["ak_out"], b * PAIRS + c)
                    pe.matmul(pj[1][:], w_qkv[:, 0, INNER + c * P:INNER + (c + 1) * P], xn[:], start=True, stop=True).then_inc(S["ak_mm"], 1)

                def project_v(t, g):
                    if t == 0:
                        pe.wait_ge(S["aq_out"] if g == 0 else S["ak_out"], b * PAIRS + 1)
                    else:
                        pe.wait_ge(S["av_out"], b * (2 * QTILES) + 2 * t + g - 1)
                    lo = 2 * INNER + g * 512
                    pe.matmul(pj[g][:], xn[:, t * P:(t + 1) * P], w_qkv[:, 0, lo:lo + 512], start=True, stop=True).then_inc(S["av_mm"], 1)

                def score(s):
                    h, qt = divmod(s, QTILES)
                    r = (h % 2) * D
                    if qt == 0 and h % 2 == 0:
                        pe.wait_ge(S["ak_out"], b * PAIRS + h // 2 + 1)
                    if s >= 2:
                        pe.wait_ge(S["a_exped"], b * A_STEPS + s - 1)
                    n = (qt + 1) * P
                    pe.matmul(ps[s % 2][:, n - P:n], identb[:], causal[:], start=True, stop=False, skip_group_check=True)
                    pe.matmul(ps[s % 2][:, 0:n], qT[r:r + D, h // 2, qt * P:n], kT[r:r + D, h // 2, 0:n],
                              start=False, stop=True, skip_group_check=True).then_inc(S["a_scored"], 1)

                def turn(s):
                    qt = s % QTILES
                    pe.wait_ge(S["a_norm"], b * A_STEPS + s + 1)
                    if s >= 2:
                        pe.wait_ge(S["a_pt_odd"] if s % 2 else S["a_pt_even"], b * (A_STEPS // 2) + s // 2)
                    for kt in range(qt + 1):
                        m = pe.transpose(pturn[s % 2][:, kt * P:(kt + 1) * P], prob[:, s % 4, kt * P:(kt + 1) * P], identf[:])
                    m.then_inc(S["a_turned"], 1)

                def weigh(h):
                    c, r = divmod(h, 2)
                    pe.wait_ge(S["a_pt_even"], b * (A_STEPS // 2) + (h + 1) * (QTILES // 2))
                    pe.wait_ge(S["a_pt_odd"], b * (A_STEPS // 2) + (h + 1) * (QTILES // 2))
                    if r == 0 and c >= 2:
                        pe.wait_ge(S["a_o_out"], b * PAIRS + c - 1)
                    for kt in range(QTILES):
                        m = pe.matmul(po[c % 2][r * D:(r + 1) * D, kt * P:SEQ], V[:, kt, h * D:(h + 1) * D],
                                      probT_a[:, h % 2, kt, kt * P:SEQ], start=(kt == 0), stop=(kt == QTILES - 1),
                                      skip_group_check=True)
                    m.then_inc(S["a_pv"], 1)

                project_qk(0)
                for t in range(QTILES):
                    for g in range(2):
                        project_v(t, g)
                for s in range(A_STEPS + 4):
                    if s < A_STEPS:
                        score(s)
                    if 2 <= s < A_STEPS + 2:
                        turn(s - 2)
                    if s % (2 * QTILES) == 3 and s // (2 * QTILES) + 1 < PAIRS:
                        project_qk(s // (2 * QTILES) + 1)
                    if s >= 4 and (s - 4) % QTILES == QTILES - 1:
                        weigh((s - 4) // QTILES)
                pe.wait_ge(S["a_o_out"], b * PAIRS + PAIRS)
                for c in range(PAIRS):
                    m = pe.matmul(pj[0][:], w_out[:, c], attnT[:, c], start=(c == 0), stop=(c == PAIRS - 1))
                m.then_inc(S["a_wo"], 1)
                mean(pj[1], b * 2 + 1)
                variance(pj[0], b * 2 + 1)

            def project_qk(n, t, c):
                if t == 0 and c == 0:
                    pe.wait_ge(S["xs_ok"], n + 1)
                    pe.wait_ge(S["wq_in"], 16 * (n // BATCH) + 16)
                if c >= 2 or t == 2:
                    pe.wait_ge(S["rotated"], n * QK_PER_ITEM + t * QK_CHUNKS + c - 1)
                elif t == 0:
                    if not first(n):
                        pe.wait_ge(S["v_out"], n * V_PER_ITEM - 1 + c)
                else:
                    pe.wait_ge(S["v_out"], n * V_PER_ITEM + (1 if t == 1 else 5) + c)
                pe.matmul(pj[c % 2][:], xs[:, t * P:(t + 1) * P], w_qkv[:, bass.ds((n // BATCH + 1) % 2, 1), c * 512:(c + 1) * 512].rearrange("p o c -> p (o c)"),
                          start=True, stop=True).then_inc(S["qk_mm"], 1)

            def project_v(n, kt):
                for g in range(2):
                    if kt in (0, 1, 3):
                        pe.wait_ge(S["rotated"], n * QK_PER_ITEM + {0: 1, 1: 3, 3: 4}[kt] * QK_CHUNKS - 1 + g)
                    else:
                        pe.wait_ge(S["v_out"], n * V_PER_ITEM + 2 * kt - 1 + g)
                    lo = 2 * INNER + g * 512
                    pe.matmul(pj[g][:], xs[:, kt * KT_STEP:kt * KT_STEP + P], w_qkv[:, bass.ds((n // BATCH + 1) % 2, 1), lo:lo + 512].rearrange("p o c -> p (o c)"),
                              start=True, stop=True).then_inc(S["v_mm"], 1)

            def turn_qk(n, t):
                pe.wait_ge(S["qk_ok"], n * QTILES + t + 1)
                for j in range(QK_CHUNKS):
                    if j >= 1 or t == 1 or (first(n) and t >= 1):
                        pe.wait_ge(S["tqk_out"], n * QK_PER_ITEM + t * QK_CHUNKS + j)
                    elif t == 0:
                        if not first(n) and not second(n):
                            pe.wait_ge(S["y2"], n - 1)
                        elif second(n):
                            pe.wait_ge(S["tqk_out"], QK_PER_ITEM)
                    elif t == 2:
                        pe.wait_ge(S["y1"], n)
                    else:
                        pe.wait_ge(S["gate_out"], (n - 1) * HCH + 2)
                    for i in range(4):
                        m = pe.transpose(px[:, i * P:(i + 1) * P],
                                         qkn[:, t % 2, (4 * j + i) * P:(4 * j + i + 1) * P], identf[:])
                    m.then_inc(S["tqk"], 1)

            def score(n, i):
                kt, g = divmod(i, GROUPS)
                if g == 0 and kt < QTILES:
                    pe.wait_ge(S["tqk_out"], n * QK_PER_ITEM + (kt + 1) * QK_CHUNKS)
                if not (first(n) and i < 2):
                    pe.wait_ge(S["exped"], n * STEPS + i - 1)
                pe.matmul(ps[i % 2][:], identb[:], band[:], start=True, stop=False, skip_group_check=True)
                r0 = kt * KT_STEP
                for j in range(4):
                    c, r = PAIRS // 2 * (g // 2) + j, (g % 2) * D
                    m = pe.matmul(ps[i % 2][:, j * P:(j + 1) * P], qT[r:r + D, c, r0:r0 + P], kT[r:r + D, c, r0:r0 + P],
                                  start=False, stop=True, skip_group_check=True)
                m.then_inc(S["scored"], 1)

            def turn(n, i):
                pe.wait_ge(S["pnorm"], n * STEPS + i + 1)
                if not (first(n) and i == 0):
                    pe.wait_ge(S["pt_out"], n * STEPS + i)
                for j in range(4):
                    m = pe.transpose(pt[:, j * P:(j + 1) * P], prob[:, i % 4, j * P:(j + 1) * P], identf[:])
                m.then_inc(S["pturned"], 1)

            def weigh(n, i):
                kt, g = divmod(i, GROUPS)
                pe.wait_ge(S["pt_out"], n * STEPS + i + 1)
                if g == 0:
                    pe.wait_ge(S["v_out"], n * V_PER_ITEM + 2 * kt + 2)
                if g % 2 == 0 and not (first(n) and kt == 0):
                    pe.wait_ge(S["o_out"], n * O_PER_ITEM + 2 * kt - 1 + g // 2)
                c0 = 0 if kt == 0 else WINDOW
                for j in range(4):
                    h = 2 * (PAIRS // 2 * (g // 2) + j) + g % 2
                    col = j * P
                    m = pe.matmul(po[g // 2][(g % 2) * D:(g % 2 + 1) * D, col + c0:col + P],
                                  V[:, kt, h * D:(h + 1) * D], probT[:, i % 2, j, c0:P],
                                  start=True, stop=True, skip_group_check=True)
                m.then_inc(S["pv_done"], 1)

            def project_out(n, half, trailing=False):
                if half == 0:
                    pe.wait_ge(S["wl_in"], (n // BATCH + 1) * WL_DMAS)
                    pe.wait_ge(S["o_out"], n * O_PER_ITEM + O_PER_ITEM)
                    if trailing:
                        pe.wait_ge(S["y2"], n)
                    else:
                        pe.wait_ge(S["tqk_out"], (n + 1) * QK_PER_ITEM + 2 * QK_CHUNKS)
                for c in range(4 * half, 4 * half + 4):
                    m = pe.matmul(px[:], w_out[:, c], attnT[:, c], start=(c == 0), stop=(c == PAIRS - 1))
                if half == 1:
                    m.then_inc(S["wo_mm"], 1)

            def ffn_mean(n, trailing=False):
                if not trailing:
                    pe.wait_ge(S["tqk_out"], (n + 1) * QK_PER_ITEM + 3 * QK_CHUNKS)
                mean(px, n + 2 * BATCH)

            def ffn_variance(n):
                variance(px, n + 2 * BATCH)

            def ffn_gate(n, i, trailing=False):
                if i == 0:
                    pe.wait_ge(S["ln_done"], n + BATCH + 1)
                elif i == 2 and not trailing:
                    pe.wait_ge(S["tqk_out"], (n + 1) * QK_PER_ITEM + 4 * QK_CHUNKS)
                else:
                    pe.wait_ge(S["gate_out"], n * HCH + i)
                lo = DIM_INNER + i * P
                pe.matmul(px[0:HROWS[i], :], w1[:, lo:lo + HROWS[i]], xn[:], start=True, stop=True).then_inc(S["gate_mm"], 1)

            def ffn_up(n, i):
                if i == 0:
                    pe.wait_ge(S["gate_out"], n * HCH + HCH)
                else:
                    pe.wait_ge(S["prod"], n * HCH + i)
                pe.matmul(px[0:HROWS[i], :], w1[:, i * P:i * P + HROWS[i]], xn[:], start=True, stop=True).then_inc(S["a_mm"], 1)

            def ffn_down(n):
                pe.wait_ge(S["prod"], n * HCH + HCH)
                for i in range(HCH):
                    m = pe.matmul(px[:], w2[0:HROWS[i], i], hidden[0:HROWS[i], i], start=(i == 0), stop=(i == HCH - 1))
                m.then_inc(S["w2_mm"], 1)

            def item(n, before=True, after=True):
                for i in range(STEPS):
                    score(n, i)
                    if i >= 2 or before:
                        turn(*at(n, i - 2))
                    if i >= 3 or before:
                        weigh(*at(n, i - 3))
                    if i == 0:
                        project_qk(n, 2, 0)
                        project_qk(n, 2, 1)
                    if i == 1:
                        turn_qk(n, 1)
                    if i == 2:
                        project_qk(n, 2, 2)
                    if i == 3:
                        project_qk(n, 2, 3)
                    if i == 4:
                        project_v(n, 1)
                        if before:
                            project_out(n - 1, 0)
                    if i == 5:
                        if before:
                            project_out(n - 1, 1)
                        turn_qk(n, 2)
                    if i == 6:
                        project_v(n, 2)
                        project_qk(n, 3, 0)
                    if i == 7:
                        project_qk(n, 3, 1)
                        if before:
                            ffn_mean(n - 1)
                    if i == 8:
                        project_qk(n, 3, 2)
                    if i == 9:
                        project_qk(n, 3, 3)
                        if before:
                            ffn_variance(n - 1)
                    if i == 10:
                        project_v(n, 3)
                    if i == 11:
                        if before:
                            ffn_gate(n - 1, 0)
                            ffn_gate(n - 1, 1)
                        turn_qk(n, 3)
                    if i == 12:
                        project_v(n, 4)
                        if before:
                            ffn_gate(n - 1, 2)
                    if i == 13 and after:
                        project_qk(n + 1, 0, 0)
                        project_qk(n + 1, 0, 1)
                    if i == 14:
                        if before:
                            ffn_up(n - 1, 0)
                        if after:
                            project_qk(n + 1, 0, 2)
                    if i == 15:
                        if before:
                            ffn_up(n - 1, 1)
                        if after:
                            project_qk(n + 1, 0, 3)
                    if i == 16:
                        if before:
                            ffn_up(n - 1, 2)
                        if after:
                            project_v(n + 1, 0)
                    if i == 17:
                        if before:
                            ffn_down(n - 1)
                        if after:
                            project_qk(n + 1, 1, 0)
                    if i == 18 and after:
                        project_qk(n + 1, 1, 1)
                        turn_qk(n + 1, 0)
                    if i == 19 and after:
                        project_qk(n + 1, 1, 2)
                        project_qk(n + 1, 1, 3)

            for c in range(QK_CHUNKS):
                project_qk(0, 0, c)
            project_v(0, 0)
            turn_qk(0, 0)
            for c in range(QK_CHUNKS):
                project_qk(0, 1, c)
            item(0, before=False)
            with pe.Fori(1, ITEMS - 1) as n:
                item(n)
            item(ITEMS - 1, after=False)
            last = ITEMS - 1
            turn(last, STEPS - 2)
            weigh(last, STEPS - 3)
            turn(last, STEPS - 1)
            weigh(last, STEPS - 2)
            weigh(last, STEPS - 1)
            project_out(last, 0, trailing=True)
            project_out(last, 1, trailing=True)
            ffn_mean(last, trailing=True)
            ffn_variance(last)
            for i in range(HCH):
                ffn_gate(last, i, trailing=True)
            for i in range(HCH):
                ffn_up(last, i)
            ffn_down(last)

            with pe.Fori(1, BATCH + 1) as b:
                pe.wait_ge(S["fin_add"], b)
                for t in range(QTILES):
                    m = pe.transpose(px[:, t * P:(t + 1) * P], xin[:, t * P:(t + 1) * P], identf[:])
                m.then_inc(S["fin_turned"], 1)

        @block.vector
        def _(dve):
            def centre(bank, k):
                dve.wait_ge(S["ln_mean"], k + 1)
                dve.tensor_tensor(xn[:], xin[:], bank[:], ALU.subtract).then_inc(S["ln_centred"], 1)

            def shifted(base, dst, done):
                dve.tensor_scalar(dst[0:D, :], yT[0:D, bass.ds(base + 1, SEQ)], 1.0, None, ALU.mult)
                dve.tensor_scalar(dst[D:P, :], yT[D:P, bass.ds(base, SEQ)], 1.0, None, ALU.mult).then_inc(done, 1)

            dve.memset(mean_w[:], 1.0 / E)
            dve.memset(eps_c[:], EPS)
            dve.memset(lift_c[:], 0.5 * float(np.log(NORM_LIFT)))
            dve.memset(hidden[:], 0.0).then_inc(S["x1_stored"], 16)
            dve.memset(yT[:], 0.0).then_inc(S["zeroed"], 1)
            dve.wait_ge(S["const_in"], 16 * N_CONST)
            dve.tensor_copy(identb[:], identf[:])
            dve.tensor_copy(causal[:], mask_f[:, 0:P])
            dve.tensor_scalar(bq[:], bq[:], 1.0 / 8.0, None, ALU.mult)
            for r in range(2):
                v = scale_d[:, r].rearrange("p (l s j) -> p l s j", s=2, j=D // 2)
                dve.tensor_copy(scale_sw[:, r].rearrange("p (l s j) -> p l s j", s=2, j=D // 2), v[:, :, ::-1, :])
            dve.tensor_copy(band[:], mask_f[:, P:5 * P]).then_inc(S["consts"], 1)
            dve.wait_ge(S["consts"], 1)
            for l in range(depth):
                for r in range(2):
                    sd = scale_d[:, r, l * D:(l + 1) * D].unsqueeze(1).to_broadcast([P, QTILES, D])
                    ss = scale_sw[:, r, l * D:(l + 1) * D].unsqueeze(1).to_broadcast([P, QTILES, D])
                    dve.tensor_tensor(tab_c[:, l, r], base_c[:, r], sd, ALU.mult)
                    m = dve.tensor_tensor(tab_s[:, l, r], base_s[:, r], ss, ALU.mult)
            m.then_inc(S["tabs"], 1)

            with dve.Fori(0, BATCH) as b:
                dve.wait_ge(S["x_turned"], b + 1)
                dve.wait_ge(S["x1_stored"], b * 16 + 16)
                dve.tensor_copy(xin[:], px[:]).then_inc(S["ln_src"], 1)
                dve.wait_ge(S["ln_src"], b * 2 + 1)
                centre(pj[1], b * 2)
                dve.wait_ge(S["ln_rstd"], b * 2 + 1)
                dve.tensor_tensor(xn[:], xn[:], rstd[:], ALU.mult).then_inc(S["ln_done"], 1)
                for s in range(A_STEPS + 2):
                    if s < A_STEPS:
                        n = (s % QTILES + 1) * P
                        dve.wait_ge(S["a_scored"], b * A_STEPS + s + 1)
                        dve.tensor_reduce(nm[:, s:s + 1], ps[s % 2][:, 0:n], AX_X, ALU.max, negate=True).then_inc(S["a_maxed"], 1)
                    if 1 <= s <= A_STEPS:
                        k = s - 1
                        n = (k % QTILES + 1) * P
                        dve.wait_ge(S["a_exped"], b * A_STEPS + k + 1)
                        dve.reciprocal(ri[:, k:k + 1], rs[:, k:k + 1]).then_inc(S["a_recip"], 1)
                        dve.wait_ge(S["a_recip"], b * A_STEPS + k + 1)
                        dve.tensor_scalar(prob[:, k % 4, 0:n], prob[:, k % 4, 0:n], ri[:, k:k + 1], None, ALU.mult).then_inc(S["a_norm"], 1)
                    if s >= 2 and s % 2 == 0:
                        k = s - 2
                        h, qt = divmod(k, QTILES)
                        n = (qt + 1) * P
                        dve.wait_ge(S["a_turned"], b * A_STEPS + k + 1)
                        if h >= 2 and qt == 0:
                            dve.wait_ge(S["a_pv"], b * HEADS + h - 1)
                        dve.tensor_copy(probT_a[:, h % 2, 0:qt + 1, qt * P:(qt + 1) * P],
                                        pturn[k % 2][:, 0:n].rearrange("p (k q) -> p k q", q=P)).then_inc(S["a_pt_even"], 1)
                dve.wait_ge(S["a_wo"], b + 1)
                dve.scalar_tensor_tensor(out=xin[:], in0=pj[0][:], scalar=b_out[:, 0:1], in1=xin[:], op0=ALU.add, op1=ALU.add).then_inc(S["ln_src"], 1)
                dve.wait_ge(S["ln_src"], b * 2 + 2)
                centre(pj[1], b * 2 + 1)
                dve.wait_ge(S["ln_rstd"], b * 2 + 2)
                dve.tensor_tensor(yT[:, bass.ds(b * YB + 1, SEQ)], xn[:], rstd[:], ALU.mult).then_inc(S["y0"], 1)

            def shift_for_qkv(n):
                if first(n):
                    dve.wait_ge(S["y0"], BATCH)
                else:
                    dve.wait_ge(S["v_mm"], n * V_PER_ITEM)
                shifted((n % BATCH) * YB, xs, S["xs_ok"])

            def rotate(n, t, c):
                u = n * QK_PER_ITEM + t * QK_CHUNKS + c
                r = c // 2
                l = n // BATCH
                dve.wait_ge(S["squared"], u + 1)
                dve.tensor_reduce(n2[:, t % 2, 8 * c:8 * c + 8], sq[:, c % 2].rearrange("p (h d) -> p h d", d=D),
                                  AX_X, ALU.add).then_inc(S["summed"], 1)
                if not (first(n) and t == 0 and c < 2):
                    dve.wait_ge(S["added"], u - 1)
                heads = pj[c % 2][:].rearrange("p (h d) -> p h d", d=D)
                swapped = pj[c % 2][:].rearrange("p (h s j) -> p h s j", s=2, j=D // 2)[:, :, ::-1, :]
                tc = tab_c[:, bass.ds(l, 1), r, t].to_broadcast([P, 8, D])
                ts = tab_s[:, bass.ds(l, 1), r, t].rearrange("p o (s j) -> p o s j", s=2).to_broadcast([P, 8, 2, D // 2])
                dve.tensor_tensor(rot_c[:, c % 2].rearrange("p (h d) -> p h d", d=D), heads, tc, ALU.mult)
                dve.tensor_tensor(rot_s[:, c % 2].rearrange("p (h s j) -> p h s j", s=2, j=D // 2),
                                  swapped, ts, ALU.mult).then_inc(S["rotated"], 1)
                if c == QK_CHUNKS - 1:
                    dve.wait_ge(S["summed"], u + 1)
                    dve.tensor_scalar(n2[:, t % 2], n2[:, t % 2], NORM_FLOOR, None, ALU.max).then_inc(S["n2_ok"], 1)

            def normalise(n, t):
                dve.wait_ge(S["rn_ok"], n * QTILES + t + 1)
                dve.wait_ge(S["added"], n * QK_PER_ITEM + (t + 1) * QK_CHUNKS)
                v = qkn[:, t % 2].rearrange("p (h d) -> p h d", d=D)
                dve.tensor_tensor(v, v, rn[:, t % 2].unsqueeze(2).to_broadcast([P, 2 * HEADS, D]), ALU.mult).then_inc(S["qk_ok"], 1)

            def row_max(n, i):
                dve.wait_ge(S["scored"], n * STEPS + i + 1)
                dve.tensor_reduce(nm[:, 4 * i:4 * i + 4], ps[i % 2][:].rearrange("p (h k) -> p h k", h=4),
                                  AX_X, ALU.max, negate=True).then_inc(S["maxed"], 1)

            def inverse_sum(n, i):
                dve.wait_ge(S["exped"], n * STEPS + i + 1)
                dve.reciprocal(ri[:, 4 * i:4 * i + 4], rs[:, 4 * i:4 * i + 4]).then_inc(S["recipd"], 1)

            def copy_turned(n, i):
                dve.wait_ge(S["pturned"], n * STEPS + i + 1)
                if not (first(n) and i < 2):
                    dve.wait_ge(S["pv_done"], n * STEPS + i - 1)
                dve.tensor_copy(probT[:, i % 2], pt[:].rearrange("p (h q) -> p h q", h=4)).then_inc(S["pt_out"], 1)

            def y_of(n):
                return yT[:, bass.ds((n % BATCH) * YB + 1, SEQ)]

            def add_attention(n):
                dve.wait_ge(S["wo_mm"], n + 1)
                dve.tensor_tensor(y_of(n), y_of(n), px[:], ALU.add).then_inc(S["y1"], 1)
                dve.wait_ge(S["y1"], n + 1)
                shifted((n % BATCH) * YB, xin, S["ln_src"])

            def ffn_centre(n):
                dve.wait_ge(S["ln_src"], n + 2 * BATCH + 1)
                centre(px, n + 2 * BATCH)

            def ffn_scale(n):
                l = n // BATCH
                dve.wait_ge(S["ln_rstd"], n + 2 * BATCH + 1)
                dve.tensor_tensor(xn[:], xn[:], rstd[:], ALU.mult).then_inc(S["ln_scaled"], 1)
                dve.wait_ge(S["ln_scaled"], n + 1)
                dve.tensor_scalar(xn[:], xn[:], ln_gb[:, 0, bass.ds(l, 1)], ln_gb[:, 1, bass.ds(l, 1)], ALU.mult, ALU.add).then_inc(S["ln_done"], 1)

            def ffn_gate(n, i):
                M = HROWS[i]
                dve.wait_ge(S["gate_mm"], n * HCH + i + 1)
                dve.tensor_scalar(hidden[0:M, i], px[0:M, :], b1[0:M, 1, i, bass.ds(n // BATCH, 1)], None, ALU.add).then_inc(S["gate_out"], 1)

            def ffn_product(n, i):
                M = HROWS[i]
                dve.wait_ge(S["gelu"], n + 1)
                dve.wait_ge(S["a_mm"], n * HCH + i + 1)
                dve.scalar_tensor_tensor(out=hidden[0:M, i], in0=px[0:M, :], scalar=b1[0:M, 0, i, bass.ds(n // BATCH, 1)],
                                         in1=hidden[0:M, i], op0=ALU.add, op1=ALU.mult).then_inc(S["prod"], 1)

            def add_ffn(n):
                dve.wait_ge(S["w2_mm"], n + 1)
                dve.scalar_tensor_tensor(out=y_of(n), in0=px[:], scalar=b2[:, bass.ds(n // BATCH, 1)], in1=y_of(n),
                                         op0=ALU.add, op1=ALU.add).then_inc(S["y2"], 1)

            def item(n, before=True, after=True):
                for i in range(STEPS):
                    row_max(n, i)
                    if i >= 1 or before:
                        inverse_sum(*at(n, i - 1))
                    if i >= 2 or before:
                        copy_turned(*at(n, i - 2))
                    if i == 0:
                        normalise(n, 1)
                        rotate(n, 2, 0)
                    if i == 1:
                        rotate(n, 2, 1)
                    if i == 2:
                        rotate(n, 2, 2)
                    if i == 3:
                        rotate(n, 2, 3)
                    if i == 4:
                        normalise(n, 2)
                    if i == 5 and before:
                        add_attention(n - 1)
                    if i == 6:
                        rotate(n, 3, 0)
                    if i == 7:
                        rotate(n, 3, 1)
                    if i == 8:
                        if before:
                            ffn_centre(n - 1)
                        rotate(n, 3, 2)
                    if i == 9:
                        rotate(n, 3, 3)
                    if i == 10:
                        normalise(n, 3)
                        if before:
                            ffn_scale(n - 1)
                    if i == 11 and before:
                        ffn_gate(n - 1, 0)
                        ffn_gate(n - 1, 1)
                    if i == 12 and before:
                        ffn_gate(n - 1, 2)
                    if i == 13:
                        if after:
                            shift_for_qkv(n + 1)
                            rotate(n + 1, 0, 0)
                    if i == 14:
                        if before:
                            ffn_product(n - 1, 0)
                        if after:
                            rotate(n + 1, 0, 1)
                    if i == 15:
                        if before:
                            ffn_product(n - 1, 1)
                        if after:
                            rotate(n + 1, 0, 2)
                    if i == 16:
                        if before:
                            ffn_product(n - 1, 2)
                        if after:
                            rotate(n + 1, 0, 3)
                    if i == 17:
                        if before:
                            add_ffn(n - 1)
                        if after:
                            normalise(n + 1, 0)
                            rotate(n + 1, 1, 0)
                    if i == 18 and after:
                        rotate(n + 1, 1, 1)
                    if i == 19 and after:
                        rotate(n + 1, 1, 2)
                        rotate(n + 1, 1, 3)

            shift_for_qkv(0)
            dve.wait_ge(S["tabs"], 1)
            for c in range(QK_CHUNKS):
                rotate(0, 0, c)
            normalise(0, 0)
            for c in range(QK_CHUNKS):
                rotate(0, 1, c)
            item(0, before=False)
            with dve.Fori(1, ITEMS - 1) as n:
                item(n)
            item(ITEMS - 1, after=False)
            last = ITEMS - 1
            inverse_sum(last, STEPS - 1)
            copy_turned(last, STEPS - 2)
            copy_turned(last, STEPS - 1)
            add_attention(last)
            ffn_centre(last)
            ffn_scale(last)
            for i in range(HCH):
                ffn_gate(last, i)
            for i in range(HCH):
                ffn_product(last, i)
            add_ffn(last)

            dve.wait_ge(S["y2"], ITEMS)
            for b in range(BATCH):
                if b >= 1:
                    dve.wait_ge(S["fin_out"], b)
                dve.wait_ge(S["x1_in"], b * 16 + 16)
                dve.tensor_tensor(xin[:], xs[:], yT[:, b * YB + 1:(b + 1) * YB], ALU.add).then_inc(S["fin_add"], 1)

        @block.scalar
        def _(act):
            def square_centred(k):
                act.wait_ge(S["ln_centred"], k + 1)
                act.activation(rstd[:], xn[:], ACT.Square).then_inc(S["ln_squared"], 1)

            def inverse_deviation(bank, k):
                act.wait_ge(S["ln_var"], k + 1)
                act.activation(rstd[:], bank[:], ACT.Ln, bias=eps_c[:, 0:1]).then_inc(S["ln_log"], 1)
                act.wait_ge(S["ln_log"], k + 1)
                act.activation(rstd[:], rstd[:], ACT.Exp, scale=-0.5).then_inc(S["ln_rstd"], 1)

            act.preload_act_table_set("natural_log_exp_and_others")
            act.wait_ge(S["zeroed"], 1)
            act.wait_ge(S["consts"], 1)
            with act.Fori(0, BATCH) as b:
                square_centred(b * 2)
                inverse_deviation(pj[0], b * 2)

                def copy_qk(c):
                    act.wait_ge(S["aq_mm"], b * PAIRS + c + 1)
                    act.activation(qT[:, c], pj[0][:], ACT.Identity, bias=bq[:, c:c + 1], scale=1.0 / 8.0).then_inc(S["aq_out"], 1)
                    act.wait_ge(S["ak_mm"], b * PAIRS + c + 1)
                    act.activation(kT[:, c], pj[1][:], ACT.Identity, bias=bk[:, c:c + 1]).then_inc(S["ak_out"], 1)

                copy_qk(0)
                for t in range(QTILES):
                    for g in range(2):
                        act.wait_ge(S["av_mm"], b * (2 * QTILES) + 2 * t + g + 1)
                        act.activation(V[:, t, g * 512:(g + 1) * 512], pj[g][:], ACT.Copy).then_inc(S["av_out"], 1)
                for s in range(A_STEPS + 5):
                    if s < A_STEPS:
                        n = (s % QTILES + 1) * P
                        act.wait_ge(S["a_maxed"], b * A_STEPS + s + 1)
                        if s >= 4:
                            act.wait_ge(S["a_turned"], b * A_STEPS + s - 3)
                        act.activation(prob[:, s % 4, 0:n], ps[s % 2][:, 0:n], ACT.Exp, bias=nm[:, s:s + 1],
                                       accum_out=rs[:, s:s + 1]).then_inc(S["a_exped"], 1)
                    if 2 <= s < A_STEPS + 2 and s % 2 == 1:
                        k = s - 2
                        h, qt = divmod(k, QTILES)
                        n = (qt + 1) * P
                        act.wait_ge(S["a_turned"], b * A_STEPS + k + 1)
                        act.activation(probT_a[:, h % 2, 0:qt + 1, qt * P:(qt + 1) * P],
                                       pturn[k % 2][:, 0:n].rearrange("p (k q) -> p k q", q=P), ACT.Copy).then_inc(S["a_pt_odd"], 1)
                    if s % (2 * QTILES) == 3 and s // (2 * QTILES) + 1 < PAIRS:
                        copy_qk(s // (2 * QTILES) + 1)
                    if s >= 5 and (s - 5) % (2 * QTILES) == 2 * QTILES - 1:
                        c = (s - 5) // (2 * QTILES)
                        act.wait_ge(S["a_pv"], b * HEADS + 2 * c + 2)
                        act.activation(attnT[:, c], po[c % 2][:], ACT.Identity, bias=bv[:, c:c + 1]).then_inc(S["a_o_out"], 1)
                square_centred(b * 2 + 1)
                inverse_deviation(pj[0], b * 2 + 1)

            def square(n, t, c):
                u = n * QK_PER_ITEM + t * QK_CHUNKS + c
                act.wait_ge(S["qk_mm"], u + 1)
                if not (first(n) and t == 0 and c < 2):
                    act.wait_ge(S["summed"], u - 1)
                act.activation(sq[:, c % 2], pj[c % 2][:], ACT.Square).then_inc(S["squared"], 1)

            def inverse_norm(n, t):
                act.wait_ge(S["n2_ok"], n * QTILES + t + 1)
                act.activation(rn[:, t % 2], n2[:, t % 2], ACT.Ln, scale=NORM_LIFT).then_inc(S["rn_log"], 1)
                act.wait_ge(S["rn_log"], n * QTILES + t + 1)
                act.activation(rn[:, t % 2], rn[:, t % 2], ACT.Exp, scale=-0.5, bias=lift_c[:, 0:1]).then_inc(S["rn_ok"], 1)

            def copy_qk(n, t):
                for j in range(QK_CHUNKS):
                    act.wait_ge(S["tqk"], n * QK_PER_ITEM + t * QK_CHUNKS + j + 1)
                    dst = (qT, kT)[j // 2]
                    act.activation(dst[:, 4 * (j % 2):4 * (j % 2) + 4, t * P:(t + 1) * P],
                                   px[:].rearrange("p (c q) -> p c q", c=4), ACT.Copy).then_inc(S["tqk_out"], 1)

            def copy_v(n, kt):
                for g in range(2):
                    act.wait_ge(S["v_mm"], n * V_PER_ITEM + 2 * kt + g + 1)
                    act.activation(V[:, kt, g * 512:(g + 1) * 512], pj[g][:], ACT.Copy).then_inc(S["v_out"], 1)

            def exponentials(n, i):
                act.wait_ge(S["maxed"], n * STEPS + i + 1)
                if not (first(n) and i < 4):
                    act.wait_ge(S["pturned"], n * STEPS + i - 3)
                for j in range(4):
                    m = act.activation(prob[:, i % 4, j * P:(j + 1) * P], ps[i % 2][:, j * P:(j + 1) * P], ACT.Exp,
                                       bias=nm[:, 4 * i + j:4 * i + j + 1], accum_out=rs[:, 4 * i + j:4 * i + j + 1])
                m.then_inc(S["exped"], 1)

            def copy_out(n, kt, half):
                act.wait_ge(S["pv_done"], n * STEPS + GROUPS * kt + 2 * half + 2)
                if kt == 0 and half == 0 and not first(n):
                    act.wait_ge(S["wo_mm"], n)
                c0 = 0 if kt == 0 else WINDOW
                act.activation(attnT[:, 4 * half:4 * half + 4, kt * KT_STEP + c0:kt * KT_STEP + P],
                               po[half][:].rearrange("p (c q) -> p c q", c=4)[:, :, c0:P], ACT.Copy).then_inc(S["o_out"], 1)

            def gelu(n):
                act.wait_ge(S["gate_out"], n * HCH + HCH)
                act.activation(hidden[:], hidden[:], ACT.Gelu).then_inc(S["gelu"], 1)
                act.preload_act_table_set("natural_log_exp_and_others")

            def item(n, before=True, after=True):
                for i in range(STEPS):
                    exponentials(n, i)
                    if i % 2 == 1 and (i >= 5 or before):
                        m, k = at(n, i - 5)
                        copy_out(m, k // GROUPS, (k % GROUPS) // 2)
                    if i == 0:
                        square(n, 2, 0)
                        square(n, 2, 1)
                    if i == 1:
                        copy_qk(n, 1)
                    if i == 2:
                        square(n, 2, 2)
                    if i == 3:
                        square(n, 2, 3)
                        inverse_norm(n, 2)
                    if i == 4:
                        copy_v(n, 1)
                    if i == 5:
                        copy_qk(n, 2)
                    if i == 6:
                        copy_v(n, 2)
                        square(n, 3, 0)
                    if i == 7:
                        square(n, 3, 1)
                    if i == 8:
                        if before:
                            square_centred(n - 1 + 2 * BATCH)
                        square(n, 3, 2)
                    if i == 9:
                        square(n, 3, 3)
                        inverse_norm(n, 3)
                        if before:
                            inverse_deviation(px, n - 1 + 2 * BATCH)
                    if i == 10:
                        copy_v(n, 3)
                    if i == 11:
                        copy_qk(n, 3)
                    if i == 12:
                        copy_v(n, 4)
                    if i == 13:
                        if before:
                            gelu(n - 1)
                        if after:
                            square(n + 1, 0, 0)
                            square(n + 1, 0, 1)
                    if i == 14 and after:
                        square(n + 1, 0, 2)
                    if i == 15 and after:
                        square(n + 1, 0, 3)
                    if i == 16 and after:
                        inverse_norm(n + 1, 0)
                        copy_v(n + 1, 0)
                    if i == 17 and after:
                        square(n + 1, 1, 0)
                    if i == 18 and after:
                        square(n + 1, 1, 1)
                        copy_qk(n + 1, 0)
                    if i == 19 and after:
                        square(n + 1, 1, 2)
                        square(n + 1, 1, 3)
                        inverse_norm(n + 1, 1)

            for c in range(QK_CHUNKS):
                square(0, 0, c)
            inverse_norm(0, 0)
            copy_v(0, 0)
            copy_qk(0, 0)
            for c in range(QK_CHUNKS):
                square(0, 1, c)
            inverse_norm(0, 1)
            item(0, before=False)
            with act.Fori(1, ITEMS - 1) as n:
                item(n)
            item(ITEMS - 1, after=False)
            last = ITEMS - 1
            copy_out(last, KTILES - 1, 0)
            copy_out(last, KTILES - 1, 1)
            square_centred(last + 2 * BATCH)
            inverse_deviation(px, last + 2 * BATCH)
            gelu(last)

            act.wait_ge(S["fin_turned"], 1)
            for b in range(BATCH):
                act.wait_ge(S["fin_turned"], b + 1)
                if b >= 1:
                    act.wait_ge(S["stored"], b * 16)
                act.activation(x_tok[:], px[:].rearrange("p (t e) -> p t e", e=E), ACT.Copy).then_inc(S["fin_out"], 1)

        @block.gpsimd
        def _(pool):
            def add(n, t, c):
                pool.wait_ge(S["rotated"], n * QK_PER_ITEM + t * QK_CHUNKS + c + 1)
                if c == 0 and not (first(n) and t < 2):
                    pool.wait_ge(S["tqk"], n * QK_PER_ITEM + (t - 1) * QK_CHUNKS)
                pool.tensor_tensor(qkn[:, t % 2, c * 512:(c + 1) * 512], rot_c[:, c % 2], rot_s[:, c % 2], ALU.add).then_inc(S["added"], 1)

            def divide(n, i):
                pool.wait_ge(S["recipd"], n * STEPS + i + 1)
                v = prob[:, i % 4].rearrange("p (h k) -> p h k", h=4)
                pool.tensor_tensor(v, v, ri[:, 4 * i:4 * i + 4].unsqueeze(2).to_broadcast([P, 4, P]), ALU.mult).then_inc(S["pnorm"], 1)

            def item(n, before=True, after=True):
                for i in range(STEPS):
                    if i >= 1 or before:
                        divide(*at(n, i - 1))
                    if i <= 3:
                        add(n, 2, i)
                    if 6 <= i <= 9:
                        add(n, 3, i - 6)
                    if 13 <= i <= 16 and after:
                        add(n + 1, 0, i - 13)
                    if 17 <= i <= 18 and after:
                        add(n + 1, 1, i - 17)
                    if i == 19 and after:
                        add(n + 1, 1, 2)
                        add(n + 1, 1, 3)

            pool.wait_ge(S["y0"], BATCH)
            for t in range(2):
                for c in range(QK_CHUNKS):
                    add(0, t, c)
            item(0, before=False)
            with pool.Fori(1, ITEMS - 1) as n:
                item(n)
            item(ITEMS - 1, after=False)
            divide(ITEMS - 1, STEPS - 1)


_INS = {'x': 'L0_attn_x', 'a_qkv_w': 'L0_attn_qkv_w', 'a_qkv_b': 'L0_attn_qkv_b', 'a_out_w': 'L0_attn_out_w',
        'a_out_b': 'L0_attn_out_b', 'Wqkv': 'L0_ffn_Wqkv', 'q_scale': 'L0_ffn_q_scale', 'k_scale': 'L0_ffn_k_scale',
        'Wo': 'L0_ffn_Wo', 'ln_g': 'L0_ffn_ln_g', 'ln_b': 'L0_ffn_ln_b', 'W1': 'L0_ffn_W1', 'b1': 'L0_ffn_b1',
        'W2': 'L0_ffn_W2', 'b2': 'L0_ffn_b2'}


def kernel(**inputs):
    import concourse.bacc as _bacc
    from concourse.bass_utils import run_bass_kernel_spmd as _run

    nc = _bacc.Bacc("TRN2", target_bir_lowering=False, num_devices=1)
    arrays, T = {}, {}

    def give(name, a):
        a = np.ascontiguousarray(a)
        arrays[f"in_{name}"] = a
        T[name] = nc.dram_tensor(f"in_{name}", a.shape, mybir.dt.from_np(a.dtype), kind="ExternalInput").ap()

    for name, full in _INS.items():
        give(name, inputs[full])
    rot_c, rot_s = rotary_constants()
    causal, band = mask_constants()
    give("rot_c", rot_c)
    give("rot_s", rot_s)
    give("masks", np.concatenate([causal, band], 1))
    give("ident", np.eye(P, dtype=np.float32))
    T["x1"] = nc.dram_tensor("x1", (BATCH, E, SEQ), F32, kind="Internal").ap()
    out = nc.dram_tensor("out_0", (BATCH, SEQ, E), F32, kind="ExternalOutput").ap()
    build(nc, T, out)
    return _run(nc, [arrays], core_ids=[0]).results[0]["out_0"]
```

```python
from contextlib import ExitStack

import numpy as np

import concourse.bass as bass
from concourse import mybir

ALU = mybir.AluOpType
ACT = mybir.ActivationFunctionType
AX_X = mybir.AxisListType.X
F32 = mybir.dt.float32
BF16 = mybir.dt.bfloat16
F32R = mybir.dt.float32r

P = 128
BATCH, SEQ, E = 8, 512, 128
HEADS, D = 16, 64
INNER = HEADS * D
PAIRS = HEADS // 2
QTILES = SEQ // P
DEPTH = 6
WINDOW = 32
DIM_INNER = int(E * 4 * 2 / 3)
HCH = -(-DIM_INNER // P)
HROWS = [min(P, DIM_INNER - P * i) for i in range(HCH)]
QK_SCALE = 8.0
EPS = 1e-5
MASKED = -1e30
LN2 = float(np.log(2.0))
NORM_FLOOR = 1e-24
NORM_LIFT = 2.0 ** 20

KT_STEP = P - WINDOW
KTILES = (SEQ - P) // KT_STEP + 1
GROUPS = HEADS // 4
STEPS = GROUPS * KTILES
QK_CHUNKS = 4
QK_PER_ITEM = QTILES * QK_CHUNKS
V_PER_ITEM = 2 * KTILES
O_PER_ITEM = 2 * KTILES
A_STEPS = HEADS * QTILES
A_CHUNKS = (0, 2, 4, 5, 1, 3)
LAYER_0_CHUNKS = (4, 5, 0, 2, 1, 3)
SPLIT_AT = {4: 0, 5: 1, 6: 2, 7: 3, 10: 4, 11: 5}
QK_A_AT = {1: 1, 10: 2, 19: 3, 27: 4, 35: 5, 43: 6, 51: 7}

QK_AT = {0: (0, 2, 2), 1: (0, 2, 3),
         2: (0, 3, 0), 3: (0, 3, 1), 4: (0, 3, 2), 5: (0, 3, 3),
         9: (1, 0, 0), 10: (1, 0, 1), 11: (1, 0, 2), 12: (1, 0, 3),
         14: (1, 1, 0), 15: (1, 1, 1), 16: (1, 1, 2), 17: (1, 1, 3),
         18: (1, 2, 0), 19: (1, 2, 1)}
V_AT = {6: (0, 2), 7: (0, 3), 8: (0, 4), 13: (1, 0), 16: (1, 1)}
NORM_AT = {19: (1, 1), 3: (0, 2), 7: (0, 3), 14: (1, 0)}
TURN_AT = {0: (0, 1, 0), 1: (0, 1, 1), 2: (0, 1, 2), 3: (0, 1, 3),
           4: (0, 2, 0), 5: (0, 2, 1), 6: (0, 2, 2), 7: (0, 2, 3),
           8: (0, 3, 0), 9: (0, 3, 1), 10: (0, 3, 2), 11: (0, 3, 3),
           16: (1, 0, 0), 17: (1, 0, 1), 18: (1, 0, 2), 19: (1, 0, 3)}

LATE = (9, 14, 19)
GATE_AT = (21, 23, 25)
UP_AT = (27, 30, 32)
GATE_OUT_AT = (10, 11, 12)
PRODUCT_AT = (14, 15, 16)


def rotary_constants():
    f = np.float32
    half = np.arange(0, D, 2, dtype=f)
    inv_freq = f(1.0) / f(10000.0) ** (half / f(D))
    t = np.arange(SEQ, dtype=f)
    freqs = t[:, None] * inv_freq[None, :]
    base_scale = (half + f(0.4 * D)) / f(1.4 * D)
    power = (t - SEQ // 2) / f(WINDOW // 2)
    scale = base_scale[None, :] ** power[:, None]
    cos, sin = np.cos(freqs), np.sin(freqs)
    inv = f(1.0) / scale
    cos_t = np.stack([cos * scale, cos * inv * f(QK_SCALE)])
    sin_t = np.stack([sin * scale, sin * inv * f(QK_SCALE)])
    return (np.concatenate([cos_t, cos_t], -1).astype(f), np.concatenate([-sin_t, sin_t], -1).astype(f))


def mask_constants():
    d = np.arange(P)[:, None] - np.arange(P)[None, :]
    causal = np.where(d >= 0, 0.0, MASKED).astype(np.float32)
    band = np.where((d >= 0) & (d <= WINDOW), 0.0, MASKED).astype(np.float32)
    return causal, np.tile(band, (1, 4))


W_CHUNKS = 3 * INNER // 512
N_CONST = 2 + 6 + 1
N_TABLE = 4 + 2 + 2 + 2 * HCH + 1
WL_DMAS = 16 * (2 + HCH)


def build(nc, T, out, depth=DEPTH):
    ITEMS = depth * BATCH
    with ExitStack() as ctx:
        def sb(name, shape, dt=F32):
            return ctx.enter_context(nc.sbuf_tensor(name, shape, dt))

        def psum(name):
            return ctx.enter_context(nc.psum_tensor(name, [P, 512], F32))

        def sem(name):
            return ctx.enter_context(nc.semaphore(name))

        YB = SEQ + 1
        yT = sb("yT", [P, BATCH * YB])
        w_hi = sb("w_hi", [P, 3 * INNER], F32R)
        w_lo = sb("w_lo", [P, 3 * INNER], F32R)
        w_out = sb("w_out", [P, PAIRS, E])
        w1 = sb("w1", [P, 2 * DIM_INNER])
        w2 = sb("w2", [P, HCH, E])
        qT = sb("qT", [P, PAIRS, SEQ])
        kT = sb("kT", [P, PAIRS, SEQ])
        V = sb("V", [P, KTILES, INNER])
        attnT = sb("attnT", [P, PAIRS, SEQ])
        qkn = sb("qkn", [P, 2, 2 * INNER])
        probT_a = qkn[:].rearrange("p a (k q) -> p (a k) q", q=SEQ)
        rot_c = sb("rot_c", [P, 2, 512])
        rot_s = sb("rot_s", [P, 2, 512])
        base_c = V[:, KTILES - 1, 0:512].rearrange("p (r t d) -> p r t d", r=2, t=QTILES)
        base_s = V[:, KTILES - 1, 512:1024].rearrange("p (r t d) -> p r t d", r=2, t=QTILES)
        mask_f = rot_c[:].rearrange("p a c -> p (a c)")[:, 0:5 * P]
        sq = sb("sq", [P, 2, 512])
        scale_d = sq[:].rearrange("p a c -> p (a c)")[:, 0:2 * DEPTH * D].rearrange("p (r c) -> p r c", r=2)
        scale_sw = rot_c[:].rearrange("p a c -> p (a c)")[:, 0:2 * DEPTH * D].rearrange("p (r c) -> p r c", r=2)
        prob = sb("prob", [P, 4, 512])
        probT = sb("probT", [P, 4, 4, P])
        hidden = sb("hidden", [P, HCH, SEQ])
        tab_c = sb("tab_c", [P, DEPTH, 2, QTILES, D])
        tab_s = sb("tab_s", [P, DEPTH, 2, QTILES, D])
        identf = sb("identf", [P, P])
        identb = sb("identb", [P, P], BF16)
        causal = sb("causal", [P, P], BF16)
        band = sb("band", [P, 4 * P], BF16)
        mean_w = sb("mean_w", [P, P])
        eps_c = sb("eps_c", [P, 1])
        lift_c = sb("lift_c", [P, 1])
        one_c = sb("one_c", [P, 1])
        bq = sb("bq", [P, PAIRS])
        bk = sb("bk", [P, PAIRS])
        bv = sb("bv", [P, PAIRS])
        b_out = sb("b_out", [P, 1])
        ln_gb = sb("ln_gb", [P, 2, DEPTH])
        b1 = sb("b1", [P, 2, HCH, DEPTH])
        b2 = sb("b2", [P, DEPTH])
        x_hi = sb("x_hi", [P, SEQ], F32R)
        x_lo = sb("x_lo", [P, SEQ], F32R)
        xs = sb("xs", [P, SEQ])
        stage1 = sb("stage1", [P, 512])
        stage_a = [rot_s[:, 0], rot_s[:, 1]]
        stage_l = [xs[:], stage1[:]]
        xin = sb("xin", [P, SEQ])
        xn = sb("xn", [P, SEQ])
        xc = hidden[:, 0]
        rstd = hidden[:, HCH - 1]
        n2 = sb("n2", [P, 2, 2 * HEADS])
        rn = sb("rn", [P, 2, 2 * HEADS])
        nm = sb("nm", [P, 4 * STEPS])
        rs = sb("rs", [P, 4 * STEPS])
        ri = sb("ri", [P, 4 * STEPS])
        x_tok = probT[:, 0]

        pj = [psum(f"pj{i}") for i in range(2)]
        pt = psum("pt")
        px = psum("px")
        ps = [psum(f"ps{i}") for i in range(2)]
        po = [psum(f"po{i}") for i in range(2)]
        pa, pf = po
        pturn = [pt, px]
        fin_sum, fin_bank, fin_tok = stage_l, [px, pt], [probT[:, 0], probT[:, 1]]

        names = """const_in consts table_in wa_in w_raw0 w_raw1 w_high w_split wl_in x_in x_turned x_copied x1_sum x_kept x1_stored x1_in0 x1_in1 zeroed x_scaled x_high
            ln_src ln_mean ln_centred ln_squared ln_var ln_log ln_rstd ln_scaled ln_done
            xs_ok qk_mm squared summed rotated added n2_ok rn_log rn_ok q_normed k_normed tqk tqk_out
            v_mm v_out scored maxed exped recipd pnorm pturned pt_out pv_done o_out wo_half y1
            gate_mm gate_out a_mm gelu prod w2_mm y2 scales tabs
            aq_mm aq_out ak_mm ak_out av_mm av_out a_scored a_maxed a_exped a_recip a_norm a_turned
            a_pt_even a_pt_odd a_pv a_o_out a_wo y0 fin_add fin_turned fin_out stored0 stored1""".split()
        S = {k: sem(k) for k in names}

        x1_in, stored = (S["x1_in0"], S["x1_in1"]), (S["stored0"], S["stored1"])

        block = ctx.enter_context(nc.Block())

        def first(n):
            return isinstance(n, int) and n == 0

        def at(n, i):
            return (n, i) if i >= 0 else (n - 1, i + STEPS)

        def at_a(b, s):
            return (b, s) if s >= 0 else (b - 1, s + A_STEPS)

        def ln_first(b):
            return 0 if first(b) else 2 * b - 1

        def ln_second(b):
            return 2 * BATCH - 1 if isinstance(b, int) and b == BATCH - 1 else 2 * b + 2

        def pair_tile(s):
            return s // (2 * QTILES), (0, 1, 3, 2)[s % (2 * QTILES) // 2]

        @block.sync
        def _(sp):
            with nc.allow_non_contiguous_dma(reason="small vectors, once"):
                sp.dma_start(x_tok[:], T["x"][0].rearrange("(t p) e -> p t e", p=P)).then_inc(S["x_in"], 16)
                c = S["const_in"]
                sp.dma_start(identf[:], T["ident"]).then_inc(c, 16)
                sp.dma_start(mask_f, T["masks"]).then_inc(c, 16)
                def load_chunk_a(pos, src):
                    if pos >= 2:
                        sp.wait_ge(S["w_split"], pos - 1)
                    dst = stage_a[pos % 2]
                    if len(src.shape) == 3:
                        dst = dst.rearrange("e (h d) -> e h d", d=D)
                    sp.dma_start(dst, src).then_inc((S["w_raw0"], S["w_raw1"])[pos % 2], 16)

                def a_chunk(c):
                    j, g = divmod(c, 2)
                    return T["a_qkv_w"][:, 8 * g:8 * g + 8, j * D:(j + 1) * D]

                for pos in range(2):
                    load_chunk_a(pos, a_chunk(A_CHUNKS[pos]))
                qkv_b = T["a_qkv_b"].rearrange("(c two) (j d) -> j two d c", two=2, j=3)
                for j, dst in enumerate((bq, bk, bv)):
                    for two in range(2):
                        sp.dma_start(dst[two * D:(two + 1) * D, :], qkv_b[j, two]).then_inc(c, 16)
                sp.dma_start(b_out[:], T["a_out_b"].unsqueeze(1)).then_inc(c, 16)
                for pos in range(2, W_CHUNKS):
                    load_chunk_a(pos, a_chunk(A_CHUNKS[pos]))
                sp.dma_start(w_out[:], T["a_out_w"].rearrange("(c two) d e -> (two d) c e", two=2)).then_inc(S["wa_in"], 16)
                c = S["table_in"]
                for r in range(2):
                    sp.dma_start(base_c[:, r], T["rot_c"][r].rearrange("(t p) d -> p t d", p=P)).then_inc(c, 16)
                    sp.dma_start(base_s[:, r], T["rot_s"][r].rearrange("(t p) d -> p t d", p=P)).then_inc(c, 16)
                for r, name in enumerate(("q_scale", "k_scale")):
                    flat = T[name].rearrange("l d -> (l d)").unsqueeze(0).to_broadcast([P, DEPTH * D])
                    sp.dma_start(scale_d[:, r], flat).then_inc(c, 16)
                sp.dma_start(ln_gb[:, 0], T["ln_g"].rearrange("l e -> e l")).then_inc(c, 16)
                sp.dma_start(ln_gb[:, 1], T["ln_b"].rearrange("l e -> e l")).then_inc(c, 16)
                for ag in range(2):
                    for i in range(HCH):
                        lo = ag * DIM_INNER + i * P
                        sp.dma_start(b1[0:HROWS[i], ag, i], T["b1"][:, lo:lo + HROWS[i]].rearrange("l e -> e l")).then_inc(c, 16)
                sp.dma_start(b2[:], T["b2"].rearrange("l e -> e l")).then_inc(c, 16)
                with sp.Fori(1, BATCH) as b:
                    sp.wait_ge(S["x_turned"], b)
                    sp.dma_start(x_tok[:], T["x"][bass.ds(b, 1)].rearrange("o (t p) e -> p (o t) e", p=P)).then_inc(S["x_in"], 16)
                    sp.wait_ge(S["x1_sum"], b)
                    sp.dma_start(T["x1"][bass.ds(b - 1, 1)].rearrange("o e s -> e (o s)"), xin[:]).then_inc(S["x1_stored"], 16)
                for pos in range(W_CHUNKS):
                    lo = LAYER_0_CHUNKS[pos] * 512
                    load_chunk_a(W_CHUNKS + pos, T["Wqkv"][0, :, lo:lo + 512])
                sp.wait_ge(S["x1_sum"], BATCH)
                sp.dma_start(T["x1"][BATCH - 1], xin[:]).then_inc(S["x1_stored"], 16)

                def load_rest(l):
                    sp.dma_start(w_out[:], T["Wo"][bass.ds(l, 1)].rearrange("o (c p) e -> p (o c) e", p=P)).then_inc(S["wl_in"], 16)
                    sp.dma_start(w1[:], T["W1"][bass.ds(l, 1)].rearrange("o e c -> e (o c)")).then_inc(S["wl_in"], 16)
                    for i in range(HCH):
                        sp.dma_start(w2[0:HROWS[i], i], T["W2"][bass.ds(l, 1), i * P:i * P + HROWS[i]].rearrange("o p e -> p (o e)")).then_inc(S["wl_in"], 16)

                sp.wait_ge(S["a_wo"], BATCH)
                load_rest(0)
                sp.wait_ge(S["y0"], BATCH)

                def load_layer(l):
                    for c in range(W_CHUNKS):
                        sp.wait_ge(S["w_split"], (l + 1) * W_CHUNKS + c - 1)
                        sp.dma_start(stage_l[c % 2], T["Wqkv"][bass.ds(l, 1), :, c * 512:(c + 1) * 512].rearrange("o e c -> e (o c)")
                                     ).then_inc((S["w_raw0"], S["w_raw1"])[c % 2], 16)
                    sp.wait_ge(S["w2_mm"], l * BATCH)
                    load_rest(l)

                if depth > 1:
                    with sp.Fori(1, depth) as l:
                        load_layer(l)
                def load_x1(b):
                    sp.dma_start(fin_sum[b % 2], T["x1"][b]).then_inc(x1_in[b % 2], 16)

                sp.wait_ge(S["x1_stored"], 16 * BATCH)
                sp.wait_ge(S["w_split"], (depth + 1) * W_CHUNKS)
                load_x1(0)
                load_x1(1)
                for b in range(BATCH):
                    if b + 2 < BATCH:
                        sp.wait_ge(S["fin_turned"], b + 1)
                        load_x1(b + 2)
                    sp.wait_ge(S["fin_out"], b + 1)
                    sp.dma_start(out[b].rearrange("(t p) e -> p t e", p=P), fin_tok[b % 2]).then_inc(stored[b % 2], 16)
                for k in range(2):
                    sp.wait_ge(stored[k], 16 * (BATCH // 2))

        @block.tensor
        def _(pe):
            def mean(bank, k, src=xin):
                pe.matmul(bank[:], mean_w[:], src[:], start=True, stop=True).then_inc(S["ln_mean"], 1)

            def variance(bank, k):
                pe.wait_ge(S["ln_squared"], k + 1)
                pe.matmul(bank[:], mean_w[:], rstd[:], start=True, stop=True).then_inc(S["ln_var"], 1)

            def product(bank, a, b):
                (a_hi, a_lo), (b_hi, b_lo) = a, b
                pe.matmul(bank, a_lo, b_hi, start=True, stop=False)
                pe.matmul(bank, a_hi, b_hi, start=False, stop=False)
                return pe.matmul(bank, a_hi, b_lo, start=False, stop=True)

            def x_part(lo, n):
                return x_hi[:, lo:lo + n], x_lo[:, lo:lo + n]

            def w_part(lo, n):
                return w_hi[:, lo:lo + n], w_lo[:, lo:lo + n]

            pe.wait_ge(S["consts"], 1)
            pe.wait_ge(S["w_split"], 2)
            pe.wait_ge(S["zeroed"], 1)

            def turn_x(b):
                pe.wait_ge(S["x_in"], b * 16 + 16)
                if not first(b):
                    pe.wait_ge(S["aq_out"], b * PAIRS)
                for t in range(QTILES):
                    m = pe.transpose(pj[0][:, t * P:(t + 1) * P], x_tok[:, t], identf[:])
                m.then_inc(S["x_turned"], 1)

            def x_mean(b):
                if not first(b):
                    pe.wait_ge(S["ak_out"], b * PAIRS)
                pe.wait_ge(S["x_copied"], b + 1)
                mean(pj[1], ln_first(b), xs)

            def project_qk_a(b, c):
                if first(b) and c == 1:
                    pe.wait_ge(S["w_split"], W_CHUNKS)
                if c == 0:
                    pe.wait_ge(S["ln_done"], b + 1)
                elif c == 2:
                    pe.wait_ge(S["av_out"], (b + 1) * (2 * QTILES) - 1)
                elif c == 3 and not first(b):
                    pe.wait_ge(S["ln_centred"], ln_second(b - 1) + 1)
                else:
                    pe.wait_ge(S["aq_out"], b * PAIRS + c)
                product(pj[0][:], w_part(c * P, P), x_part(0, SEQ)).then_inc(S["aq_mm"], 1)
                if c == 2:
                    pe.wait_ge(S["av_out"], (b + 1) * (2 * QTILES))
                elif c == 3 and not first(b):
                    pe.wait_ge(S["ln_log"], ln_second(b - 1) + 1)
                elif c > 0:
                    pe.wait_ge(S["ak_out"], b * PAIRS + c)
                product(pj[1][:], w_part(INNER + c * P, P), x_part(0, SEQ)).then_inc(S["ak_mm"], 1)

            def project_v_a(b, t):
                for g in range(2):
                    if t == 0:
                        pe.wait_ge(S["aq_out"] if g == 0 else S["ak_out"], b * PAIRS + 2)
                    else:
                        pe.wait_ge(S["av_out"], b * (2 * QTILES) + 2 * t + g - 1)
                    lo = 2 * INNER + g * 512
                    product(pj[g][:], x_part(t * P, P), w_part(lo, 512)).then_inc(S["av_mm"], 1)

            def score_a(b, s):
                c, qt = pair_tile(s)
                r = (s % 2) * D
                if s % (2 * QTILES) == 0:
                    pe.wait_ge(S["ak_out"], b * PAIRS + c + 1)
                if not (first(b) and s < 2):
                    pe.wait_ge(S["a_exped"], b * A_STEPS + s - 1)
                n = (qt + 1) * P
                pe.matmul(ps[s % 2][:, n - P:n], identb[:], causal[:], start=True, stop=False, skip_group_check=True)
                pe.matmul(ps[s % 2][:, 0:n], qT[r:r + D, c, qt * P:n], kT[r:r + D, c, 0:n],
                          start=False, stop=True, skip_group_check=True).then_inc(S["a_scored"], 1)

            def turn_a(b, s):
                qt = pair_tile(s)[1]
                pe.wait_ge(S["a_norm"], b * A_STEPS + s + 1)
                if not (first(b) and s < 2):
                    pe.wait_ge(S["a_pt_odd"] if s % 2 else S["a_pt_even"], b * (A_STEPS // 2) + s // 2)
                for kt in range(qt + 1):
                    m = pe.transpose(pturn[s % 2][:, kt * P:(kt + 1) * P], prob[:, s % 4, kt * P:(kt + 1) * P], identf[:])
                m.then_inc(S["a_turned"], 1)

            def weigh_a(b, s):
                c, qt = pair_tile(s)
                pe.wait_ge(S["a_pt_even"], b * (A_STEPS // 2) + s // 2 + 1)
                pe.wait_ge(S["a_pt_odd"], b * (A_STEPS // 2) + s // 2 + 1)
                if c == 0:
                    pe.wait_ge(S["av_out"], b * (2 * QTILES) + 2 * qt + 2)
                if s % (2 * QTILES) == 0:
                    if not (first(b) and c < 2):
                        pe.wait_ge(S["a_o_out"], b * PAIRS + c - 1)
                    if c == 1 and not first(b):
                        pe.wait_ge(S["x1_sum"], b)
                for kt in range(qt + 1):
                    for r in range(2):
                        h = 2 * c + r
                        m = pe.matmul(po[c % 2][r * D:(r + 1) * D, qt * P:(qt + 1) * P], V[:, kt, h * D:(h + 1) * D],
                                      probT_a[:, (s + r) % 8, kt * P:(kt + 1) * P], start=(kt == 0), stop=(kt == qt),
                                      skip_group_check=True)
                m.then_inc(S["a_pv"], 1)

            def project_out_a(b, c):
                if c == 0:
                    pe.wait_ge(S["wa_in"], 16)
                    pe.wait_ge(S["a_o_out"], b * PAIRS + PAIRS)
                m = pe.matmul(po[1][:], w_out[:, c], attnT[:, c], start=(c == 0), stop=(c == PAIRS - 1))
                if c == PAIRS - 1:
                    m.then_inc(S["a_wo"], 1)

            def sequence(b, before=True, after=True):
                for s in range(A_STEPS):
                    score_a(b, s)
                    if 5 <= s < 5 + QTILES:
                        project_v_a(b, s - 5)
                    if s >= 3 or before:
                        turn_a(*at_a(b, s - 3))
                    if s % 2 == 0 and (s >= 6 or before):
                        weigh_a(*at_a(b, s - 6))
                    if s in QK_A_AT:
                        project_qk_a(b, QK_A_AT[s])
                    if before:
                        if 6 <= s < 10:
                            project_out_a(b - 1, 2 * (s - 6))
                            project_out_a(b - 1, 2 * (s - 6) + 1)
                        if s == 12:
                            pe.wait_ge(S["aq_out"], b * PAIRS + 3)
                            pe.wait_ge(S["x1_sum"], b)
                            mean(pj[0], ln_second(b - 1))
                        if s == 14:
                            pe.wait_ge(S["ak_out"], b * PAIRS + 3)
                            variance(pj[1], ln_second(b - 1))
                    if after:
                        if s == 53:
                            turn_x(b + 1)
                        if s == 54:
                            x_mean(b + 1)
                        if s == 58:
                            variance(pj[0], ln_first(b + 1))
                        if s == 61:
                            project_qk_a(b + 1, 0)

            turn_x(0)
            x_mean(0)
            variance(pj[0], ln_first(0))
            project_qk_a(0, 0)
            sequence(0, before=False)
            with pe.Fori(1, BATCH - 1) as b:
                sequence(b)
            sequence(BATCH - 1, after=False)
            for s in range(A_STEPS - 3, A_STEPS):
                turn_a(BATCH - 1, s)
            for s in range(A_STEPS - 6, A_STEPS, 2):
                weigh_a(BATCH - 1, s)
            for c in range(PAIRS):
                project_out_a(BATCH - 1, c)
            pe.wait_ge(S["x1_sum"], BATCH)
            mean(pj[0], ln_second(BATCH - 1))
            variance(pj[1], ln_second(BATCH - 1))

            def project_qk(n, t, c):
                if t == 0 and c == 0:
                    pe.wait_ge(S["xs_ok"], n + 1)
                if t == 0:
                    pe.wait_ge(S["w_split"], 2 * W_CHUNKS if first(n) else (n // BATCH + 1) * W_CHUNKS + c + 1)
                if t == 0 and c < 2:
                    if first(n):
                        pe.wait_ge((S["ln_centred"], S["ln_log"])[c], 2 * BATCH)
                    else:
                        pe.wait_ge(S["v_out"], n * V_PER_ITEM - 1 + c)
                elif t == 1:
                    pe.wait_ge(S["v_out"], n * V_PER_ITEM + 1 + c)
                else:
                    pe.wait_ge(S["rotated"], n * QK_PER_ITEM + t * QK_CHUNKS + c - 1)
                product(pj[c % 2][:], x_part(t * P, P), w_part(c * 512, 512)).then_inc(S["qk_mm"], 1)

            def project_v(n, kt):
                for g in range(2):
                    if kt < 3:
                        before = {0: QK_CHUNKS, 1: QK_CHUNKS + 2, 2: 4 * QK_CHUNKS}[kt]
                        pe.wait_ge(S["rotated"], n * QK_PER_ITEM + before - 1 + g)
                    else:
                        pe.wait_ge(S["v_out"], n * V_PER_ITEM + 2 * kt - 1 + g)
                    if kt == 0 and not first(n):
                        pe.wait_ge(S["w_split"], (n // BATCH + 1) * W_CHUNKS + 5 + g)
                    lo = 2 * INNER + g * 512
                    product(pj[g][:], x_part(kt * KT_STEP, P), w_part(lo, 512)).then_inc(S["v_mm"], 1)

            def turn_qk(n, t, j):
                if j < 2:
                    pe.wait_ge(S["q_normed"], n * QTILES + t + 1)
                else:
                    pe.wait_ge(S["k_normed"], n * (2 * QTILES) + 2 * t + j - 1)
                if not (first(n) and t == 0 and j == 0):
                    pe.wait_ge(S["tqk_out"], n * QK_PER_ITEM + t * QK_CHUNKS + j)
                for i in range(4):
                    m = pe.transpose(px[:, i * P:(i + 1) * P], qkn[:, t % 2, (4 * j + i) * P:(4 * j + i + 1) * P], identf[:])
                m.then_inc(S["tqk"], 1)

            def score(n, i):
                kt, g = divmod(i, GROUPS)
                if g == 0 and kt < QTILES:
                    pe.wait_ge(S["tqk_out"], n * QK_PER_ITEM + (kt + 1) * QK_CHUNKS)
                if not (first(n) and i < 2):
                    pe.wait_ge(S["exped"], n * STEPS + i - 1)
                pe.matmul(ps[i % 2][:], identb[:], band[:], start=True, stop=False, skip_group_check=True)
                r0 = kt * KT_STEP
                for j in range(4):
                    c, r = PAIRS // 2 * (g // 2) + j, (g % 2) * D
                    m = pe.matmul(ps[i % 2][:, j * P:(j + 1) * P], qT[r:r + D, c, r0:r0 + P], kT[r:r + D, c, r0:r0 + P],
                                  start=False, stop=True, skip_group_check=True)
                m.then_inc(S["scored"], 1)

            def turn(n, i):
                pe.wait_ge(S["pnorm"], n * STEPS + i + 1)
                if not (first(n) and i == 0):
                    pe.wait_ge(S["pt_out"], n * STEPS + i)
                for j in range(4):
                    m = pe.transpose(pt[:, j * P:(j + 1) * P], prob[:, i % 4, j * P:(j + 1) * P], identf[:])
                m.then_inc(S["pturned"], 1)

            def weigh(n, i):
                late = 1 - i % 2
                n, k = at(n, i - late)
                kt, g = divmod(k, GROUPS)
                if not late:
                    pe.wait_ge(S["pt_out"], n * STEPS + k + 1)
                    if g == 1:
                        pe.wait_ge(S["v_out"], n * V_PER_ITEM + 2 * kt + 2)
                    if not (first(n) and k == 1):
                        pe.wait_ge(S["o_out"], n * O_PER_ITEM + k // 2)
                c0 = 0 if kt == 0 else WINDOW
                for j in range(2 * late, 2 * late + 2):
                    for r in range(2):
                        h = 2 * (PAIRS // 2 * (g // 2) + j) + r
                        m = pe.matmul(pa[r * D:(r + 1) * D, j * P + c0:(j + 1) * P],
                                      V[:, kt, h * D:(h + 1) * D], probT[:, (k - 1 + r) % 4, j, c0:P],
                                      start=True, stop=True, skip_group_check=True)
                if late:
                    m.then_inc(S["pv_done"], 1)

            def project_out(n, c):
                if c == 0:
                    pe.wait_ge(S["wl_in"], (n // BATCH + 1) * WL_DMAS)
                    if not first(n):
                        pe.wait_ge(S["y2"], n)
                if c % 4 == 0:
                    pe.wait_ge(S["o_out"], n * O_PER_ITEM + O_PER_ITEM - 1 + c // 4)
                m = pe.matmul(pf[:], w_out[:, c], attnT[:, c], start=(c == 0), stop=(c == PAIRS - 1))
                if c % 4 == 3:
                    m.then_inc(S["wo_half"], 1)

            def ffn_gate(n, i):
                if i == 0:
                    pe.wait_ge(S["ln_done"], n + BATCH + 1)
                else:
                    pe.wait_ge(S["gate_out"], n * HCH + i)
                lo = DIM_INNER + i * P
                pe.matmul(pf[0:HROWS[i], :], w1[:, lo:lo + HROWS[i]], xn[:], start=True, stop=True).then_inc(S["gate_mm"], 1)

            def ffn_up(n, i):
                if i == 0:
                    pe.wait_ge(S["gate_out"], n * HCH + HCH)
                else:
                    pe.wait_ge(S["prod"], n * HCH + i)
                pe.matmul(pf[0:HROWS[i], :], w1[:, i * P:i * P + HROWS[i]], xn[:], start=True, stop=True).then_inc(S["a_mm"], 1)

            def ffn_down(n, i):
                if i == 0:
                    pe.wait_ge(S["prod"], n * HCH + HCH)
                m = pe.matmul(pf[:], w2[0:HROWS[i], i], hidden[0:HROWS[i], i], start=(i == 0), stop=(i == HCH - 1))
                if i == HCH - 1:
                    m.then_inc(S["w2_mm"], 1)

            def ffn_share(n, i, half):
                k = 2 * i + half
                if 4 <= k < 4 + PAIRS:
                    project_out(n - 1, k - 4)
                if k == 14:
                    pe.wait_ge(S["ln_src"], n)
                    mean(pf, n - 1 + 2 * BATCH)
                if k == 16:
                    variance(pf, n - 1 + 2 * BATCH)
                if k in GATE_AT:
                    ffn_gate(n - 1, GATE_AT.index(k))
                if k in UP_AT:
                    ffn_up(n - 1, UP_AT.index(k))
                if 36 <= k < 36 + HCH:
                    ffn_down(n - 1, k - 36)

            def item(n, before=True, after=True):
                def is_on(table, i):
                    return i in table and (after or not table[i][0])

                for i in range(STEPS):
                    score(n, i)
                    if is_on(TURN_AT, i):
                        o, t, j = TURN_AT[i]
                        turn_qk(n + o, t, j)
                    late = i in V_AT or i in LATE
                    if is_on(QK_AT, i) and not late:
                        o, t, c = QK_AT[i]
                        project_qk(n + o, t, c)
                    if is_on(V_AT, i) and i in QK_AT:
                        o, kt = V_AT[i]
                        project_v(n + o, kt)
                    if before:
                        ffn_share(n, i, 0)
                    if i >= 2 or before:
                        turn(*at(n, i - 2))
                    if i >= 4 or before:
                        weigh(*at(n, i - 3))
                    if is_on(QK_AT, i) and late:
                        o, t, c = QK_AT[i]
                        project_qk(n + o, t, c)
                    if is_on(V_AT, i) and i not in QK_AT:
                        o, kt = V_AT[i]
                        project_v(n + o, kt)
                    if before:
                        ffn_share(n, i, 1)

            for c in range(QK_CHUNKS):
                project_qk(0, 0, c)
            project_v(0, 0)
            for j in range(QK_CHUNKS):
                turn_qk(0, 0, j)
            project_qk(0, 1, 0)
            project_qk(0, 1, 1)
            project_v(0, 1)
            project_qk(0, 1, 2)
            project_qk(0, 1, 3)
            project_qk(0, 2, 0)
            project_qk(0, 2, 1)
            item(0, before=False)
            with pe.Fori(1, ITEMS - 1) as n:
                item(n)
            item(ITEMS - 1, after=False)
            last = ITEMS - 1
            turn(last, STEPS - 2)
            weigh(last, STEPS - 3)
            turn(last, STEPS - 1)
            weigh(last, STEPS - 2)
            weigh(last, STEPS - 1)
            weigh(ITEMS, 0)

            def turn_out(b):
                pe.wait_ge(S["fin_add"], b + 1)
                if b >= 2:
                    pe.wait_ge(S["fin_out"], b - 1)
                for t in range(QTILES):
                    m = pe.transpose(fin_bank[b % 2][:, t * P:(t + 1) * P], fin_sum[b % 2][:, t * P:(t + 1) * P], identf[:])
                m.then_inc(S["fin_turned"], 1)

            halves = [(i, half) for i in range(STEPS) for half in range(2)]
            for b, (lo, hi) in enumerate(((0, 12), (12, 15), (15, 17), (17, 22), (22, 26), (26, 28), (28, 34), (34, 40))):
                for i, half in halves[lo:hi]:
                    ffn_share(ITEMS, i, half)
                turn_out(b)

        @block.vector
        def _(dve):
            def centre(bank, k, src=xin, dst=xn):
                dve.wait_ge(S["ln_mean"], k + 1)
                dve.tensor_tensor(dst[:], src[:], bank[:], ALU.subtract).then_inc(S["ln_centred"], 1)

            def shifted(base, dst, done):
                dve.tensor_scalar(dst[0:D, :], yT[0:D, bass.ds(base + 1, SEQ)], 1.0, None, ALU.mult)
                dve.tensor_scalar(dst[D:P, :], yT[D:P, bass.ds(base, SEQ)], 1.0, None, ALU.mult).then_inc(done, 1)

            dve.memset(mean_w[:], 1.0 / E)
            dve.memset(eps_c[:], EPS)
            dve.memset(one_c[:], 1.0)
            dve.memset(lift_c[:], 0.5 * float(np.log(NORM_LIFT)))
            dve.memset(hidden[:], 0.0)
            dve.memset(yT[:], 0.0).then_inc(S["zeroed"], 1)
            dve.wait_ge(S["const_in"], 16 * N_CONST)
            dve.tensor_copy(identb[:], identf[:])
            dve.tensor_copy(causal[:], mask_f[:, 0:P])
            dve.tensor_scalar(bq[:], bq[:], 1.0 / 8.0, None, ALU.mult)
            dve.tensor_copy(band[:], mask_f[:, P:5 * P]).then_inc(S["consts"], 1)
            def shift_for_qkv(n):
                if first(n):
                    dve.wait_ge(S["ak_mm"], BATCH * PAIRS)
                    dve.wait_ge(S["y0"], 1)
                else:
                    dve.wait_ge(S["v_mm"], n * V_PER_ITEM)
                base = (n % BATCH) * YB
                shifted(base, x_hi, S["x_high"])
                dve.wait_ge(S["x_high"], n + BATCH + 1)
                dve.tensor_tensor(x_lo[0:D, :], yT[0:D, bass.ds(base + 1, SEQ)], x_hi[0:D, :], ALU.subtract)
                dve.tensor_tensor(x_lo[D:P, :], yT[D:P, bass.ds(base, SEQ)], x_hi[D:P, :], ALU.subtract).then_inc(S["xs_ok"], 1)

            def take_x(b):
                dve.wait_ge(S["x_turned"], b + 1)
                dve.tensor_copy(xs[:], pj[0][:]).then_inc(S["x_copied"], 1)

            def x_centre(b):
                dve.wait_ge(S["x_copied"], b + 1)
                centre(pj[1], ln_first(b), src=xs)

            def x_scale(b):
                dve.wait_ge(S["ln_rstd"], ln_first(b) + 1)
                dve.tensor_tensor(xn[:], xn[:], rstd[:], ALU.mult).then_inc(S["x_scaled"], 1)
                dve.wait_ge(S["x_scaled"], b + 1)
                dve.tensor_scalar(x_hi[:], xn[:], 1.0, None, ALU.mult).then_inc(S["x_high"], 1)
                dve.wait_ge(S["x_high"], b + 1)
                dve.tensor_tensor(x_lo[:], xn[:], x_hi[:], ALU.subtract).then_inc(S["ln_done"], 1)

            def keep_x(b):
                if not first(b):
                    dve.wait_ge(S["x1_stored"], b * 16)
                dve.tensor_scalar(xin[:], xs[:], 1.0, None, ALU.mult).then_inc(S["x_kept"], 1)

            def row_max_a(b, s):
                n = (pair_tile(s)[1] + 1) * P
                dve.wait_ge(S["a_scored"], b * A_STEPS + s + 1)
                dve.tensor_reduce(nm[:, s:s + 1], ps[s % 2][:, 0:n], AX_X, ALU.max, negate=True).then_inc(S["a_maxed"], 1)

            def divide_a(b, s):
                n = (pair_tile(s)[1] + 1) * P
                dve.wait_ge(S["a_exped"], b * A_STEPS + s + 1)
                dve.reciprocal(ri[:, s:s + 1], rs[:, s:s + 1]).then_inc(S["a_recip"], 1)
                dve.wait_ge(S["a_recip"], b * A_STEPS + s + 1)
                dve.tensor_scalar(prob[:, s % 4, 0:n], prob[:, s % 4, 0:n], ri[:, s:s + 1], None, ALU.mult).then_inc(S["a_norm"], 1)

            def copy_turned_a(b, s):
                n = (pair_tile(s)[1] + 1) * P
                dve.wait_ge(S["a_turned"], b * A_STEPS + s + 1)
                if not (first(b) and s < 8):
                    dve.wait_ge(S["a_pv"], b * (A_STEPS // 2) + s // 2 - 3)
                dve.tensor_scalar(probT_a[:, s % 8, 0:n], pturn[0][:, 0:n], 1.0, None, ALU.mult).then_inc(S["a_pt_even"], 1)

            def add_x(b):
                dve.wait_ge(S["a_wo"], b + 1)
                dve.wait_ge(S["x_kept"], b + 1)
                dve.scalar_tensor_tensor(out=xin[:], in0=po[1][:], scalar=b_out[:, 0:1], in1=xin[:], op0=ALU.add, op1=ALU.add).then_inc(S["x1_sum"], 1)

            def y_scale(b):
                dve.wait_ge(S["ln_rstd"], ln_second(b) + 1)
                dve.tensor_tensor(yT[:, bass.ds(b * YB + 1, SEQ)], xc, rstd, ALU.mult).then_inc(S["y0"], 1)

            def sequence(b, before=True, after=True):
                for s in range(A_STEPS):
                    row_max_a(b, s)
                    if s >= 1 or before:
                        divide_a(*at_a(b, s - 1))
                    if s % 2 == 1 and (s >= 3 or before):
                        copy_turned_a(*at_a(b, s - 3))
                    if before:
                        if s == 10:
                            add_x(b - 1)
                        if s == 13:
                            dve.wait_ge(S["x1_sum"], b)
                            centre(pj[0], ln_second(b - 1), dst=xc)
                        if s == 16:
                            y_scale(b - 1)
                    if s == 20:
                        keep_x(b)
                    if after:
                        if s == 53:
                            take_x(b + 1)
                        if s == 55:
                            x_centre(b + 1)
                        if s == 60:
                            x_scale(b + 1)

            take_x(0)
            x_centre(0)
            x_scale(0)
            sequence(0, before=False)
            with dve.Fori(1, BATCH - 1) as b:
                sequence(b)
            sequence(BATCH - 1, after=False)
            divide_a(BATCH - 1, A_STEPS - 1)
            copy_turned_a(BATCH - 1, A_STEPS - 2)
            shift_for_qkv(0)
            add_x(BATCH - 1)
            dve.wait_ge(S["x1_sum"], BATCH)
            centre(pj[0], ln_second(BATCH - 1), dst=xc)
            y_scale(BATCH - 1)

            def rotate(n, t, c):
                u = n * QK_PER_ITEM + t * QK_CHUNKS + c
                r = c // 2
                l = n // BATCH
                dve.wait_ge(S["squared"], u + 1)
                dve.tensor_reduce(n2[:, t % 2, 8 * c:8 * c + 8], sq[:, c % 2].rearrange("p (h d) -> p h d", d=D),
                                  AX_X, ALU.add).then_inc(S["summed"], 1)
                if not (first(n) and t == 0 and c < 2):
                    dve.wait_ge(S["added"], u - 1)
                heads = pj[c % 2][:].rearrange("p (h d) -> p h d", d=D)
                swapped = pj[c % 2][:].rearrange("p (h s j) -> p h s j", s=2, j=D // 2)[:, :, ::-1, :]
                tc = tab_c[:, bass.ds(l, 1), r, t].to_broadcast([P, 8, D])
                ts = tab_s[:, bass.ds(l, 1), r, t].rearrange("p o (s j) -> p o s j", s=2).to_broadcast([P, 8, 2, D // 2])
                dve.tensor_tensor(rot_c[:, c % 2].rearrange("p (h d) -> p h d", d=D), heads, tc, ALU.mult)
                dve.tensor_tensor(rot_s[:, c % 2].rearrange("p (h s j) -> p h s j", s=2, j=D // 2),
                                  swapped, ts, ALU.mult).then_inc(S["rotated"], 1)
                if c == QK_CHUNKS - 1:
                    dve.wait_ge(S["summed"], u + 1)
                    dve.tensor_scalar(n2[:, t % 2], n2[:, t % 2], NORM_FLOOR, None, ALU.max).then_inc(S["n2_ok"], 1)

            def normalise(n, t):
                dve.wait_ge(S["rn_ok"], n * QTILES + t + 1)
                dve.wait_ge(S["added"], n * QK_PER_ITEM + t * QK_CHUNKS + 2)
                v = qkn[:, t % 2, 0:INNER].rearrange("p (h d) -> p h d", d=D)
                dve.tensor_tensor(v, v, rn[:, t % 2, 0:HEADS].unsqueeze(2).to_broadcast([P, HEADS, D]), ALU.mult).then_inc(S["q_normed"], 1)

            def row_max(n, i):
                dve.wait_ge(S["scored"], n * STEPS + i + 1)
                dve.tensor_reduce(nm[:, 4 * i:4 * i + 4], ps[i % 2][:].rearrange("p (h k) -> p h k", h=4),
                                  AX_X, ALU.max, negate=True).then_inc(S["maxed"], 1)

            def inverse_sum(n, i):
                dve.wait_ge(S["exped"], n * STEPS + i + 1)
                dve.reciprocal(ri[:, 4 * i:4 * i + 4], rs[:, 4 * i:4 * i + 4]).then_inc(S["recipd"], 1)

            def copy_turned(n, i):
                dve.wait_ge(S["pturned"], n * STEPS + i + 1)
                if not (first(n) and i < 4):
                    dve.wait_ge(S["pv_done"], n * (STEPS // 2) + i // 2 - 1)
                dve.tensor_copy(probT[:, i % 4], pt[:].rearrange("p (h q) -> p h q", h=4)).then_inc(S["pt_out"], 1)

            def y_of(n):
                return yT[:, bass.ds((n % BATCH) * YB + 1, SEQ)]

            def add_attention(n):
                dve.wait_ge(S["wo_half"], 2 * n + 2)
                dve.tensor_tensor(y_of(n), y_of(n), pf[:], ALU.add).then_inc(S["y1"], 1)
                dve.wait_ge(S["y1"], n + 1)
                shifted((n % BATCH) * YB, xin, S["ln_src"])

            def ffn_centre(n):
                dve.wait_ge(S["ln_src"], n + 1)
                centre(pf, n + 2 * BATCH)

            def ffn_scale(n):
                l = n // BATCH
                dve.wait_ge(S["ln_rstd"], n + 2 * BATCH + 1)
                dve.tensor_tensor(xn[:], xn[:], rstd[:], ALU.mult).then_inc(S["ln_scaled"], 1)
                dve.wait_ge(S["ln_scaled"], n + 1)
                dve.tensor_scalar(xn[:], xn[:], ln_gb[:, 0, bass.ds(l, 1)], ln_gb[:, 1, bass.ds(l, 1)], ALU.mult, ALU.add).then_inc(S["ln_done"], 1)

            def ffn_product(n, i):
                M = HROWS[i]
                dve.wait_ge(S["gelu"], n + 1)
                dve.wait_ge(S["a_mm"], n * HCH + i + 1)
                dve.scalar_tensor_tensor(out=hidden[0:M, i], in0=pf[0:M, :], scalar=b1[0:M, 0, i, bass.ds(n // BATCH, 1)],
                                         in1=hidden[0:M, i], op0=ALU.add, op1=ALU.mult).then_inc(S["prod"], 1)

            def add_ffn(n):
                dve.wait_ge(S["w2_mm"], n + 1)
                dve.scalar_tensor_tensor(out=y_of(n), in0=pf[:], scalar=b2[:, bass.ds(n // BATCH, 1)], in1=y_of(n),
                                         op0=ALU.add, op1=ALU.add).then_inc(S["y2"], 1)

            def item(n, before=True, after=True):
                for i in range(STEPS):
                    row_max(n, i)
                    if i >= 1 or before:
                        inverse_sum(*at(n, i - 1))
                    if i >= 2 or before:
                        copy_turned(*at(n, i - 2))
                    if i in NORM_AT and (after or not NORM_AT[i][0]):
                        o, t = NORM_AT[i]
                        normalise(n + o, t)
                    if i == 8 and after:
                        shift_for_qkv(n + 1)
                    if before:
                        if i == 6:
                            add_attention(n - 1)
                        if i == 7:
                            ffn_centre(n - 1)
                        if i == 9:
                            ffn_scale(n - 1)
                        if i in PRODUCT_AT:
                            ffn_product(n - 1, PRODUCT_AT.index(i))
                        if i == 19:
                            add_ffn(n - 1)
                    if i in QK_AT and (after or not QK_AT[i][0]):
                        o, t, c = QK_AT[i]
                        rotate(n + o, t, c)

            dve.wait_ge(S["tabs"], 1)
            for c in range(QK_CHUNKS):
                rotate(0, 0, c)
            normalise(0, 0)
            for c in range(QK_CHUNKS):
                rotate(0, 1, c)
            normalise(0, 1)
            rotate(0, 2, 0)
            rotate(0, 2, 1)
            item(0, before=False)
            with dve.Fori(1, ITEMS - 1) as n:
                item(n)
            item(ITEMS - 1, after=False)
            last = ITEMS - 1
            inverse_sum(last, STEPS - 1)
            copy_turned(last, STEPS - 2)
            copy_turned(last, STEPS - 1)

            def add_out(b):
                dve.wait_ge(x1_in[b % 2], 16 * (b // 2 + 1))
                dve.wait_ge(S["y2"], ITEMS - BATCH + b + 1)
                dve.tensor_tensor(fin_sum[b % 2], fin_sum[b % 2], yT[:, b * YB + 1:(b + 1) * YB], ALU.add).then_inc(S["fin_add"], 1)

            add_attention(last)
            add_out(0)
            add_out(1)
            ffn_centre(last)
            add_out(2)
            ffn_scale(last)
            add_out(3)
            add_out(4)
            add_out(5)
            ffn_product(last, 0)
            ffn_product(last, 1)
            ffn_product(last, 2)
            add_out(6)
            add_ffn(last)
            add_out(7)

        @block.scalar
        def _(act):
            def square_centred(k, src=xn):
                act.wait_ge(S["ln_centred"], k + 1)
                act.activation(rstd[:], src[:], ACT.Square).then_inc(S["ln_squared"], 1)

            def inverse_deviation(bank, k):
                act.wait_ge(S["ln_var"], k + 1)
                act.activation(rstd[:], bank[:], ACT.Ln, bias=eps_c[:, 0:1]).then_inc(S["ln_log"], 1)
                act.wait_ge(S["ln_log"], k + 1)
                act.activation(rstd[:], rstd[:], ACT.Exp, scale=-0.5).then_inc(S["ln_rstd"], 1)

            act.preload_act_table_set("natural_log_exp_and_others")
            act.wait_ge(S["zeroed"], 1)
            act.wait_ge(S["consts"], 1)

            def copy_qk_a(b, c):
                act.wait_ge(S["aq_mm"], b * PAIRS + c + 1)
                act.activation(qT[:, c], pj[0][:], ACT.Identity, bias=bq[:, c:c + 1], scale=1.0 / 8.0).then_inc(S["aq_out"], 1)
                act.wait_ge(S["ak_mm"], b * PAIRS + c + 1)
                act.activation(kT[:, c], pj[1][:], ACT.Identity, bias=bk[:, c:c + 1]).then_inc(S["ak_out"], 1)

            def copy_v_a(b, t):
                for g in range(2):
                    act.wait_ge(S["av_mm"], b * (2 * QTILES) + 2 * t + g + 1)
                    act.activation(V[:, t, g * 512:(g + 1) * 512], pj[g][:], ACT.Copy).then_inc(S["av_out"], 1)

            def exponentials_a(b, s):
                n = (pair_tile(s)[1] + 1) * P
                act.wait_ge(S["a_maxed"], b * A_STEPS + s + 1)
                if not (first(b) and s < 4):
                    act.wait_ge(S["a_turned"], b * A_STEPS + s - 3)
                act.activation(prob[:, s % 4, 0:n], ps[s % 2][:, 0:n], ACT.Exp, bias=nm[:, s:s + 1],
                               accum_out=rs[:, s:s + 1]).then_inc(S["a_exped"], 1)

            def copy_turned_a(b, s):
                n = (pair_tile(s)[1] + 1) * P
                act.wait_ge(S["a_turned"], b * A_STEPS + s + 1)
                if not (first(b) and s < 8):
                    act.wait_ge(S["a_pv"], b * (A_STEPS // 2) + s // 2 - 3)
                act.activation(probT_a[:, s % 8, 0:n], pturn[1][:, 0:n], ACT.Copy).then_inc(S["a_pt_odd"], 1)

            def copy_out_a(b, c):
                act.wait_ge(S["a_pv"], b * (A_STEPS // 2) + QTILES * (c + 1))
                if c == 0 and not first(b):
                    act.wait_ge(S["a_wo"], b)
                act.activation(attnT[:, c], po[c % 2][:], ACT.Identity, bias=bv[:, c:c + 1]).then_inc(S["a_o_out"], 1)

            def sequence(b, before=True, after=True):
                for s in range(A_STEPS):
                    exponentials_a(b, s)
                    if s % 2 == 0 and (s >= 4 or before):
                        copy_turned_a(*at_a(b, s - 3))
                    if s % 8 == 5 and (s > 5 or before):
                        m, k = at_a(b, s - 13)
                        copy_out_a(m, k // 8)
                    if 5 <= s < 5 + QTILES:
                        copy_v_a(b, s - 5)
                    if before:
                        if s == 13:
                            square_centred(ln_second(b - 1), src=xc)
                        if s == 15:
                            inverse_deviation(pj[1], ln_second(b - 1))
                    if s in QK_A_AT:
                        copy_qk_a(b, QK_A_AT[s])
                    if after:
                        if s == 56:
                            square_centred(ln_first(b + 1))
                        if s == 59:
                            inverse_deviation(pj[0], ln_first(b + 1))
                        if s == 62:
                            copy_qk_a(b + 1, 0)

            square_centred(ln_first(0))
            inverse_deviation(pj[0], ln_first(0))
            copy_qk_a(0, 0)
            sequence(0, before=False)
            with act.Fori(1, BATCH - 1) as b:
                sequence(b)
            sequence(BATCH - 1, after=False)
            copy_turned_a(BATCH - 1, A_STEPS - 3)
            copy_turned_a(BATCH - 1, A_STEPS - 1)
            copy_out_a(BATCH - 1, PAIRS - 1)
            square_centred(ln_second(BATCH - 1), src=xc)
            inverse_deviation(pj[1], ln_second(BATCH - 1))

            def square(n, t, c):
                u = n * QK_PER_ITEM + t * QK_CHUNKS + c
                act.wait_ge(S["qk_mm"], u + 1)
                if not (first(n) and t == 0 and c < 2):
                    act.wait_ge(S["summed"], u - 1)
                act.activation(sq[:, c % 2], pj[c % 2][:], ACT.Square).then_inc(S["squared"], 1)

            def inverse_norm(n, t):
                act.wait_ge(S["n2_ok"], n * QTILES + t + 1)
                act.activation(rn[:, t % 2], n2[:, t % 2], ACT.Ln, scale=NORM_LIFT).then_inc(S["rn_log"], 1)
                act.wait_ge(S["rn_log"], n * QTILES + t + 1)
                act.activation(rn[:, t % 2], rn[:, t % 2], ACT.Exp, scale=-0.5, bias=lift_c[:, 0:1]).then_inc(S["rn_ok"], 1)

            def copy_qk(n, t, j):
                act.wait_ge(S["tqk"], n * QK_PER_ITEM + t * QK_CHUNKS + j + 1)
                dst = (qT, kT)[j // 2]
                act.activation(dst[:, 4 * (j % 2):4 * (j % 2) + 4, t * P:(t + 1) * P],
                               px[:].rearrange("p (c q) -> p c q", c=4), ACT.Copy).then_inc(S["tqk_out"], 1)

            def copy_v(n, kt):
                for g in range(2):
                    act.wait_ge(S["v_mm"], n * V_PER_ITEM + 2 * kt + g + 1)
                    act.activation(V[:, kt, g * 512:(g + 1) * 512], pj[g][:], ACT.Copy).then_inc(S["v_out"], 1)

            def exponentials(n, i):
                act.wait_ge(S["maxed"], n * STEPS + i + 1)
                if not (first(n) and i < 4):
                    act.wait_ge(S["pturned"], n * STEPS + i - 3)
                for j in range(4):
                    m = act.activation(prob[:, i % 4, j * P:(j + 1) * P], ps[i % 2][:, j * P:(j + 1) * P], ACT.Exp,
                                       bias=nm[:, 4 * i + j:4 * i + j + 1], accum_out=rs[:, 4 * i + j:4 * i + j + 1])
                m.then_inc(S["exped"], 1)

            def copy_out(n, i):
                act.wait_ge(S["pv_done"], n * (STEPS // 2) + i // 2 + 1)
                kt, half = i // GROUPS, (i % GROUPS) // 2
                if kt == 0 and not first(n):
                    act.wait_ge(S["wo_half"], 2 * n - 1 + half)
                c0 = 0 if kt == 0 else WINDOW
                act.activation(attnT[:, 4 * half:4 * half + 4, kt * KT_STEP + c0:kt * KT_STEP + P],
                               pa[:].rearrange("p (c q) -> p c q", c=4)[:, :, c0:P], ACT.Copy).then_inc(S["o_out"], 1)

            def ffn_gate(n, i):
                M = HROWS[i]
                act.wait_ge(S["gate_mm"], n * HCH + i + 1)
                act.activation(hidden[0:M, i], pf[0:M, :], ACT.Identity, bias=b1[0:M, 1, i, bass.ds(n // BATCH, 1)]).then_inc(S["gate_out"], 1)

            def gelu(n):
                act.wait_ge(S["gate_out"], n * HCH + HCH)
                act.activation(hidden[:], hidden[:], ACT.Gelu).then_inc(S["gelu"], 1)
                act.preload_act_table_set("natural_log_exp_and_others")

            def ffn_share(n, i):
                if i == 7:
                    square_centred(n - 1 + 2 * BATCH)
                if i == 8:
                    inverse_deviation(pf, n - 1 + 2 * BATCH)
                if i in GATE_OUT_AT:
                    ffn_gate(n - 1, GATE_OUT_AT.index(i))
                if i == 12:
                    gelu(n - 1)

            def item(n, before=True, after=True):
                def is_on(table, i):
                    return i in table and (after or not table[i][0])

                for i in range(STEPS):
                    late = i in V_AT or i in LATE
                    if is_on(TURN_AT, i):
                        o, t, j = TURN_AT[i]
                        copy_qk(n + o, t, j)
                    if is_on(QK_AT, i) and not late:
                        o, t, c = QK_AT[i]
                        square(n + o, t, c)
                    exponentials(n, i)
                    if is_on(V_AT, i) and i in QK_AT:
                        o, kt = V_AT[i]
                        copy_v(n + o, kt)
                    if is_on(QK_AT, i - 1) and QK_AT[i - 1][2] == QK_CHUNKS - 1:
                        o, t, c = QK_AT[i - 1]
                        inverse_norm(n + o, t)
                    if i % 2 == 1 and (i >= 5 or before):
                        copy_out(*at(n, i - 4))
                    if is_on(QK_AT, i) and late:
                        o, t, c = QK_AT[i]
                        square(n + o, t, c)
                    if before:
                        ffn_share(n, i)
                    if is_on(V_AT, i) and i not in QK_AT:
                        o, kt = V_AT[i]
                        copy_v(n + o, kt)

            for c in range(QK_CHUNKS):
                square(0, 0, c)
            inverse_norm(0, 0)
            copy_v(0, 0)
            for j in range(QK_CHUNKS):
                copy_qk(0, 0, j)
            square(0, 1, 0)
            square(0, 1, 1)
            copy_v(0, 1)
            square(0, 1, 2)
            square(0, 1, 3)
            inverse_norm(0, 1)
            square(0, 2, 0)
            square(0, 2, 1)
            item(0, before=False)
            with act.Fori(1, ITEMS - 1) as n:
                item(n)
            item(ITEMS - 1, after=False)
            copy_out(ITEMS - 1, STEPS - 3)
            copy_out(ITEMS - 1, STEPS - 1)

            def copy_result(b):
                act.wait_ge(S["fin_turned"], b + 1)
                if b >= 2:
                    act.wait_ge(stored[b % 2], 16 * (b // 2))
                act.activation(fin_tok[b % 2], fin_bank[b % 2][:].rearrange("p (t e) -> p t e", e=E), ACT.Copy).then_inc(S["fin_out"], 1)

            for b, (lo, hi) in enumerate(((0, 0), (0, 8), (8, 9), (9, 11), (11, 12), (12, 20), (20, 20), (20, 20))):
                for i in range(lo, hi):
                    ffn_share(ITEMS, i)
                copy_result(b)

        @block.gpsimd
        def _(pool):
            def add(n, t, c):
                pool.wait_ge(S["rotated"], n * QK_PER_ITEM + t * QK_CHUNKS + c + 1)
                if not (first(n) and t < 2):
                    pool.wait_ge(S["tqk"], n * QK_PER_ITEM + (t - 2) * QK_CHUNKS + c + 1)
                pool.tensor_tensor(qkn[:, t % 2, c * 512:(c + 1) * 512], rot_c[:, c % 2], rot_s[:, c % 2], ALU.add).then_inc(S["added"], 1)

            def divide(n, i):
                pool.wait_ge(S["recipd"], n * STEPS + i + 1)
                v = prob[:, i % 4].rearrange("p (h k) -> p h k", h=4)
                pool.tensor_tensor(v, v, ri[:, 4 * i:4 * i + 4].unsqueeze(2).to_broadcast([P, 4, P]), ALU.mult).then_inc(S["pnorm"], 1)

            def normalise(n, t):
                pool.wait_ge(S["rn_ok"], n * QTILES + t + 1)
                pool.wait_ge(S["added"], n * QK_PER_ITEM + (t + 1) * QK_CHUNKS)
                for c in range(2):
                    lo = INNER + c * 512
                    v = qkn[:, t % 2, lo:lo + 512].rearrange("p (h d) -> p h d", d=D)
                    pool.tensor_tensor(v, v, rn[:, t % 2, HEADS + 8 * c:HEADS + 8 * c + 8].unsqueeze(2).to_broadcast([P, 8, D]),
                                       ALU.mult).then_inc(S["k_normed"], 1)

            def item(n, before=True, after=True, layer=None):
                for i in range(STEPS):
                    if i >= 1 or before:
                        divide(*at(n, i - 1))
                    if i in NORM_AT and (after or not NORM_AT[i][0]):
                        o, t = NORM_AT[i]
                        normalise(n + o, t)
                    if i in QK_AT and (after or not QK_AT[i][0]):
                        o, t, c = QK_AT[i]
                        add(n + o, t, c)
                    if layer is not None and i in SPLIT_AT:
                        c = SPLIT_AT[i]
                        if c < 4:
                            pool.wait_ge(S["qk_mm"], n * QK_PER_ITEM + 3 * QK_CHUNKS + c + 1)
                        else:
                            pool.wait_ge(S["v_mm"], n * V_PER_ITEM + V_PER_ITEM)
                        split(layer + 1, c, c, stage_l)

            def split(g, pos, c, stage):
                lo = c * 512
                pool.wait_ge((S["w_raw0"], S["w_raw1"])[pos % 2], 16 * (g * (W_CHUNKS // 2) + pos // 2 + 1))
                pool.tensor_tensor(w_hi[:, lo:lo + 512], stage[pos % 2], one_c[:, 0:1].to_broadcast([P, 512]), ALU.mult).then_inc(S["w_high"], 1)
                pool.wait_ge(S["w_high"], g * W_CHUNKS + pos + 1)
                pool.tensor_tensor(w_lo[:, lo:lo + 512], stage[pos % 2], w_hi[:, lo:lo + 512], ALU.subtract).then_inc(S["w_split"], 1)

            pool.wait_ge(S["zeroed"], 1)
            for pos in range(W_CHUNKS):
                split(0, pos, A_CHUNKS[pos], stage_a)
            pool.wait_ge(S["table_in"], 16 * N_TABLE)
            pool.wait_ge(S["consts"], 1)
            for r in range(2):
                v = scale_d[:, r].rearrange("p (l s j) -> p l s j", s=2, j=D // 2)
                m = pool.tensor_scalar(scale_sw[:, r].rearrange("p (l s j) -> p l s j", s=2, j=D // 2), v[:, :, ::-1, :], 1.0, None, ALU.mult)
            m.then_inc(S["scales"], 1)
            pool.wait_ge(S["scales"], 1)
            for l in range(depth):
                for r in range(2):
                    sd = scale_d[:, r, l * D:(l + 1) * D].unsqueeze(1).to_broadcast([P, QTILES, D])
                    ss = scale_sw[:, r, l * D:(l + 1) * D].unsqueeze(1).to_broadcast([P, QTILES, D])
                    pool.tensor_tensor(tab_c[:, l, r], base_c[:, r], sd, ALU.mult)
                    m = pool.tensor_tensor(tab_s[:, l, r], base_s[:, r], ss, ALU.mult)
            m.then_inc(S["tabs"], 1)
            for pos, c in enumerate(LAYER_0_CHUNKS):
                if c >= 4:
                    pool.wait_ge(S["av_mm"], BATCH * 2 * QTILES)
                else:
                    pool.wait_ge((S["aq_mm"], S["ak_mm"])[c // 2], (BATCH - 1) * PAIRS + PAIRS // 2 * (c % 2 + 1))
                split(1, pos, c, stage_a)

            pool.wait_ge(S["y0"], BATCH)
            for t in range(2):
                for c in range(QK_CHUNKS):
                    add(0, t, c)
                if t == 0:
                    normalise(0, 0)
            normalise(0, 1)
            add(0, 2, 0)
            add(0, 2, 1)
            item(0, before=False)
            with pool.Fori(1, BATCH - 1) as n:
                item(n)
            if depth > 1:
                item(BATCH - 1, layer=1)
                if depth > 2:
                    with pool.Fori(1, depth - 1) as l:
                        with pool.Fori(0, BATCH - 1) as j:
                            item(l * BATCH + j)
                        item(l * BATCH + BATCH - 1, layer=l + 1)
                with pool.Fori(ITEMS - BATCH, ITEMS - 1) as n:
                    item(n)
            item(ITEMS - 1, after=False)
            divide(ITEMS - 1, STEPS - 1)


_INS = {'x': 'L0_attn_x', 'a_qkv_w': 'L0_attn_qkv_w', 'a_qkv_b': 'L0_attn_qkv_b', 'a_out_w': 'L0_attn_out_w',
        'a_out_b': 'L0_attn_out_b', 'Wqkv': 'L0_ffn_Wqkv', 'q_scale': 'L0_ffn_q_scale', 'k_scale': 'L0_ffn_k_scale',
        'Wo': 'L0_ffn_Wo', 'ln_g': 'L0_ffn_ln_g', 'ln_b': 'L0_ffn_ln_b', 'W1': 'L0_ffn_W1', 'b1': 'L0_ffn_b1',
        'W2': 'L0_ffn_W2', 'b2': 'L0_ffn_b2'}


def kernel(**inputs):
    import concourse.bacc as _bacc
    from concourse.bass_utils import run_bass_kernel_spmd as _run

    nc = _bacc.Bacc("TRN2", target_bir_lowering=False, num_devices=1)
    arrays, T = {}, {}

    def give(name, a):
        a = np.ascontiguousarray(a)
        arrays[f"in_{name}"] = a
        T[name] = nc.dram_tensor(f"in_{name}", a.shape, mybir.dt.from_np(a.dtype), kind="ExternalInput").ap()

    for name, full in _INS.items():
        give(name, inputs[full])
    rot_c, rot_s = rotary_constants()
    causal, band = mask_constants()
    give("rot_c", rot_c)
    give("rot_s", rot_s)
    give("masks", np.concatenate([causal, band], 1))
    give("ident", np.eye(P, dtype=np.float32))
    T["x1"] = nc.dram_tensor("x1", (BATCH, E, SEQ), F32, kind="Internal").ap()
    out = nc.dram_tensor("out_0", (BATCH, SEQ, E), F32, kind="ExternalOutput").ap()
    build(nc, T, out)
    return _run(nc, [arrays], core_ids=[0]).results[0]["out_0"]
```
